# Optimizing a Trainium2 kernel written in Bass

```python
import numpy as np
import jax
import jax.numpy as jnp

def _softmax(x, axis=-1):
    return jax.nn.softmax(x, axis=axis)
def _gelu(x):
    return jax.nn.gelu(x, approximate=True)
def _silu(x):
    return jax.nn.silu(x)
def _sigmoid(x):
    return jax.nn.sigmoid(x)
def _layernorm(x, axis=-1, eps=1e-5):
    m = jnp.mean(x, axis=axis, keepdims=True)
    v = jnp.var(x, axis=axis, keepdims=True)
    return (x - m) / jnp.sqrt(v + eps)
def _scatter_add(tgt, idx, src, axis=0):
    return tgt.at[idx].add(src)
def _segment_sum(src, seg, n):
    return jax.ops.segment_sum(src, seg, n)

kernel_name = 'mk_conv_seq_d1_conv_nhwc256_a1ae2d'

def setup_inputs(seed: int = 0):
    np.random.seed(seed)
    _w = jnp.asarray
    def _rec_inputs():
        import jax
        import jax.numpy as jnp
        _gk = jax.random.key(seed)
        x = -0.0003972 + 0.9999 * jax.random.normal(jax.random.fold_in(_gk, 1), (8, 80, 80, 256), jnp.float32)
        return x
    x = _rec_inputs()
    def _L0_conv_setup():
        import jax, jax.numpy as jnp
        import numpy as np
        DIM = 256
        HEADS = 8
        EXP = 2

        def layer_norm(x, g, b, eps=1e-05):
            mu = jnp.mean(x, axis=-1, keepdims=True)
            var = jnp.var(x, axis=-1, keepdims=True)
            return (x - mu) * jax.lax.rsqrt(var + eps) * g + b

        def retention(q, k, v, decay_h, decay_w, num_heads):
            B, H, W, C = q.shape
            hd = C // num_heads
            q = q.reshape(B, H, W, num_heads, hd).transpose(0, 3, 1, 2, 4)
            k = k.reshape(B, H, W, num_heads, hd).transpose(0, 3, 1, 2, 4)
            v = v.reshape(B, H, W, num_heads, hd).transpose(0, 3, 1, 2, 4)
            qk_h = jnp.einsum('bnhwc,bnHwc->bnhHw', q, k)
            qk_h = qk_h * decay_h[None, :, :, :, None]
            out_h = jnp.einsum('bnhHw,bnHwc->bnhwc', qk_h, v)
            qk_w = jnp.einsum('bnhwc,bnhWc->bnhwW', q, k)
            qk_w = qk_w * decay_w[None, :, None, :, :]
            out_w = jnp.einsum('bnhwW,bnhWc->bnhwc', qk_w, v)
            out = (out_h + out_w) * 0.5
            return out.transpose(0, 2, 3, 1, 4).reshape(B, H, W, C)
        key = jax.random.key(seed)
        ks = jax.random.split(key, 10)
        B, H, W, C = (8, 80, 80, DIM)
        s = 0.02
        return {'x': jax.random.normal(ks[0], (B, H, W, C), jnp.float32), 'decay_h': jax.random.uniform(ks[1], (HEADS, H, H), jnp.float32), 'decay_w': jax.random.uniform(ks[2], (HEADS, W, W), jnp.float32), 'qkv_w': jax.random.normal(ks[3], (C, 3 * C), jnp.float32) * s, 'qkv_b': jnp.zeros((3 * C,), jnp.float32), 'proj_w': jax.random.normal(ks[4], (C, C), jnp.float32) * s, 'proj_b': jnp.zeros((C,), jnp.float32), 'ln1_g': jnp.ones((C,), jnp.float32), 'ln1_b': jnp.zeros((C,), jnp.float32), 'ln2_g': jnp.ones((C,), jnp.float32), 'ln2_b': jnp.zeros((C,), jnp.float32), 'ffn_w1': jax.random.normal(ks[5], (C, EXP * C), jnp.float32) * s, 'ffn_b1': jnp.zeros((EXP * C,), jnp.float32), 'ffn_w2': jax.random.normal(ks[6], (EXP * C, C), jnp.float32) * s, 'ffn_b2': jnp.zeros((C,), jnp.float32), 'gamma': jnp.ones((C,), jnp.float32)}
    _L0_conv_all = _L0_conv_setup()
    _L0_conv_in = {k: v for k, v in _L0_conv_all.items() if k in ('decay_h', 'decay_w', 'qkv_w', 'qkv_b', 'proj_w', 'proj_b', 'ln1_g', 'ln1_b', 'ln2_g', 'ln2_b', 'ffn_w1', 'ffn_b1', 'ffn_w2', 'ffn_b2', 'gamma', )}
    del _L0_conv_all

    return {
        "x": x,
        "L0_conv_decay_h": _L0_conv_in["decay_h"],
        "L0_conv_decay_w": _L0_conv_in["decay_w"],
        "L0_conv_qkv_w": _L0_conv_in["qkv_w"],
        "L0_conv_qkv_b": _L0_conv_in["qkv_b"],
        "L0_conv_proj_w": _L0_conv_in["proj_w"],
        "L0_conv_proj_b": _L0_conv_in["proj_b"],
        "L0_conv_ln1_g": _L0_conv_in["ln1_g"],
        "L0_conv_ln1_b": _L0_conv_in["ln1_b"],
        "L0_conv_ln2_g": _L0_conv_in["ln2_g"],
        "L0_conv_ln2_b": _L0_conv_in["ln2_b"],
        "L0_conv_ffn_w1": _L0_conv_in["ffn_w1"],
        "L0_conv_ffn_b1": _L0_conv_in["ffn_b1"],
        "L0_conv_ffn_w2": _L0_conv_in["ffn_w2"],
        "L0_conv_ffn_b2": _L0_conv_in["ffn_b2"],
        "L0_conv_gamma": _L0_conv_in["gamma"],
    }

def reference(x, L0_conv_decay_h, L0_conv_decay_w, L0_conv_qkv_w, L0_conv_qkv_b, L0_conv_proj_w, L0_conv_proj_b, L0_conv_ln1_g, L0_conv_ln1_b, L0_conv_ln2_g, L0_conv_ln2_b, L0_conv_ffn_w1, L0_conv_ffn_b1, L0_conv_ffn_w2, L0_conv_ffn_b2, L0_conv_gamma):
    import jax
    import jax.numpy as jnp
    def _L0_conv_ref(x, decay_h, decay_w, qkv_w, qkv_b, proj_w, proj_b, ln1_g, ln1_b, ln2_g, ln2_b, ffn_w1, ffn_b1, ffn_w2, ffn_b2, gamma):
        import jax, jax.numpy as jnp
        import numpy as np
        DIM = 256
        HEADS = 8
        EXP = 2

        def layer_norm(x, g, b, eps=1e-05):
            mu = jnp.mean(x, axis=-1, keepdims=True)
            var = jnp.var(x, axis=-1, keepdims=True)
            return (x - mu) * jax.lax.rsqrt(var + eps) * g + b

        def retention(q, k, v, decay_h, decay_w, num_heads):
            B, H, W, C = q.shape
            hd = C // num_heads
            q = q.reshape(B, H, W, num_heads, hd).transpose(0, 3, 1, 2, 4)
            k = k.reshape(B, H, W, num_heads, hd).transpose(0, 3, 1, 2, 4)
            v = v.reshape(B, H, W, num_heads, hd).transpose(0, 3, 1, 2, 4)
            qk_h = jnp.einsum('bnhwc,bnHwc->bnhHw', q, k)
            qk_h = qk_h * decay_h[None, :, :, :, None]
            out_h = jnp.einsum('bnhHw,bnHwc->bnhwc', qk_h, v)
            qk_w = jnp.einsum('bnhwc,bnhWc->bnhwW', q, k)
            qk_w = qk_w * decay_w[None, :, None, :, :]
            out_w = jnp.einsum('bnhwW,bnhWc->bnhwc', qk_w, v)
            out = (out_h + out_w) * 0.5
            return out.transpose(0, 2, 3, 1, 4).reshape(B, H, W, C)
        residual = x
        h = layer_norm(x, ln1_g, ln1_b)
        qkv = h @ qkv_w + qkv_b
        q, k, v = jnp.split(qkv, 3, axis=-1)
        h = retention(q, k, v, decay_h, decay_w, HEADS)
        h = h @ proj_w + proj_b
        x = residual + h * gamma
        residual = x
        h = layer_norm(x, ln2_g, ln2_b)
        h = jax.nn.gelu(h @ ffn_w1 + ffn_b1, approximate=False) @ ffn_w2 + ffn_b2
        return residual + h

    def _gn(v, G=32, eps=1e-5):
        B_, H_, W_, C_ = v.shape
        g = v.reshape(B_, H_, W_, G, C_ // G)
        m = jnp.mean(g, axis=(1, 2, 4), keepdims=True)
        s = jnp.var(g, axis=(1, 2, 4), keepdims=True)
        return ((g - m) / jnp.sqrt(s + eps)).reshape(v.shape)

    def _ln_c(v, eps=1e-6):
        m = jnp.mean(v, axis=-1, keepdims=True)
        s = jnp.var(v, axis=-1, keepdims=True)
        return (v - m) / jnp.sqrt(s + eps)

    def _ln_t(v, eps=1e-5):
        m = jnp.mean(v, axis=-1, keepdims=True)
        s = jnp.var(v, axis=-1, keepdims=True)
        return (v - m) / jnp.sqrt(s + eps)

    def _to_tokens(v):
        B_, H_, W_, C_ = v.shape
        return v.reshape(B_, H_ * W_, C_)
    def _from_tokens(t, like):
        return t.reshape(like.shape)

    x = _L0_conv_ref(x, L0_conv_decay_h, L0_conv_decay_w, L0_conv_qkv_w, L0_conv_qkv_b, L0_conv_proj_w, L0_conv_proj_b, L0_conv_ln1_g, L0_conv_ln1_b, L0_conv_ln2_g, L0_conv_ln2_b, L0_conv_ffn_w1, L0_conv_ffn_b1, L0_conv_ffn_w2, L0_conv_ffn_b2, L0_conv_gamma)
    return x


_drawn_inputs = setup_inputs


def setup_inputs(seed=0):
    import zlib

    import numpy as np

    out = dict(_drawn_inputs(seed))
    spreads = {'L0_conv_qkv_b': (0.0, 0.1),
     'L0_conv_proj_b': (0.0, 0.1),
     'L0_conv_ln1_g': (1.0, 0.2),
     'L0_conv_ln1_b': (0.0, 0.1),
     'L0_conv_ln2_g': (1.0, 0.6),
     'L0_conv_ln2_b': (0.0, 0.8),
     'L0_conv_ffn_b1': (0.0, 0.353),
     'L0_conv_ffn_b2': (0.0, 0.1),
     'L0_conv_gamma': (1.0, 0.2)}
    factors = {}
    for name, (base, spread) in spreads.items():
        noise = np.random.default_rng([zlib.crc32(name.encode()), seed]).standard_normal(out[name].shape)
        drawn = base * np.exp(spread * noise) if base else spread * noise
        out[name] = jnp.asarray(drawn.astype(out[name].dtype))
    for name, factor in factors.items():
        out[name] = (out[name] * factor).astype(out[name].dtype)
    return out
```

```python
from contextlib import ExitStack

import concourse.bass as bass
from concourse import mybir

ALU = mybir.AluOpType
ACT = mybir.ActivationFunctionType
F32 = mybir.dt.float32
F32R = mybir.dt.float32r
I32 = mybir.dt.int32
ds = bass.ds

P = 128
HEADS = 8
EPS = 1e-5
RSQRT_SEED = float(0x5F3759DF)
NEWTON_STEPS = 3


def shifted(unit, k):
    half, par = unit
    return half + (par + k) // 2, (par + k) % 2


def index(unit):
    return 2 * unit[0] + unit[1]


def run_slots(eng, slot, count, back, ahead):
    first = back + back % 2
    last = (count - ahead) // 2 * 2

    def straight(units):
        for s in units:
            slot((s // 2, s % 2), lambda k: 0 <= s + k < count)

    straight(range(-ahead, first))
    with eng.Fori(first // 2, last // 2) as half:
        for par in range(2):
            slot((half, par), lambda k: True)
    straight(range(last, count + back))


def build(nc, x, decay_h, decay_w, qkv_w, qkv_b, proj_w, proj_b, ln1_g, ln1_b, ln2_g, ln2_b,
          ffn_w1, ffn_b1, ffn_w2, ffn_b2, gamma, v_rows, out):
    B, H, W, C = x.shape
    assert H == W and C == 2 * P and H % 8 == 0
    N = H * W
    KC = C // P
    HD = C // HEADS
    HG = HEADS // KC
    FF = ffn_w1.shape[1]
    KF = FF // P
    T = 2
    STRIP = T * P
    STRIPS = N // STRIP
    LINES = 4
    CH = LINES * W
    CHUNKS = H // LINES
    COMBOS = [(g, d) for g in range(KC) for d in range(2)]
    CHUNKS_IMG = len(COMBOS) * CHUNKS
    assert N % STRIP == 0 and CHUNKS % 2 == 0 and HD == 32

    with ExitStack() as ctx:
        def sb(name, shape, dt=F32):
            return ctx.enter_context(nc.sbuf_tensor(name, shape, dt))

        def sem(name):
            return ctx.enter_context(nc.semaphore(name))

        q_img = sb("q_img", [P, KC, N])
        k_img = sb("k_img", [P, KC, N])
        out_h = sb("out_h", [P, N])
        TW = T * C
        x_in = out_h[:, 0:2 * TW].rearrange("p (u t c) -> p u t c", u=2, t=T)
        x_norm = out_h[:, 2 * TW:4 * TW].rearrange("p (u t c) -> p u t c", u=2, t=T)
        x_mid = out_h[:, 4 * TW:6 * TW].rearrange("p (u t c) -> p u t c", u=2, t=T)
        stage = out_h[:, 6 * TW:8 * TW].rearrange("p (u t c) -> p u t c", u=2, t=T)
        act_f = out_h[:, 8 * TW:8 * TW + KF * STRIP].rearrange("p (k n) -> p k n", k=KF)
        w_qkv = sb("w_qkv", [P, 2, KC, 3 * C], F32R)
        w_proj = sb("w_proj", [P, 2, KC, C], F32R)
        w_up = sb("w_up", [P, 2, KC, FF], F32R)
        w_down = sb("w_down", [P, 2, KF, C], F32R)
        h_t = sb("h_t", [P, 2, 2, KC, STRIP], F32R)
        ret_t = sb("ret_t", [P, 2, KC, STRIP], F32R)
        act_t = sb("act_t", [P, 2, KF, STRIP], F32R)
        decay = sb("decay", [H, 2, KC, HG * H])
        ident = sb("ident", [P, P])
        v_bias = sb("v_bias", [P, C])
        proj_bias = sb("proj_bias", [P, C])
        down_bias = sb("down_bias", [P, C])
        qk_bias = sb("qk_bias", [P, 2 * KC])
        up_bias = sb("up_bias", [P, KF])
        q_blocks = sb("q_blocks", [P, 2, HG, CH])
        k_chunk = sb("k_chunk", [P, 2, CH])
        v_chunk = sb("v_chunk", [H, 2, LINES, P])
        probs = sb("probs", [H, LINES, HG * H])
        bn = sb("bn", [P, 2, T, 6])
        mean_var = sb("mean_var", [P, 2, T, 2])
        var_eps = sb("var_eps", [P, 2, T])
        neg_half = sb("neg_half", [P, 2, T])
        rstd = sb("rstd", [P, 2, T])
        newton = sb("newton", [P, 2, T])
        three_halves = sb("three_halves", [P, T])

        bank = [ctx.enter_context(nc.psum_tensor(f"bank{i}", [P, 512], F32)) for i in range(8)]
        t_bank = bank[0:2]
        q_bank, k_bank, v_bank = (bank[2], bank[5]), (bank[3], bank[6]), (bank[4], bank[7])
        proj_bank, up_bank, down_bank = bank[5:7], bank[2:4], (bank[4], bank[7])
        s_bank, o_bank = bank[0:4], bank[4:6]

        w_in, dw_in = sem("w_in"), sem("dw_in")
        ident_clear, ident_done = sem("ident_clear"), sem("ident_done")
        setup_v, setup_pe, setup_ready = sem("setup_v"), sem("setup_pe"), sem("setup_ready")
        setup_link = sem("setup_link")
        xa_in = [sem(f"xa_in{u}") for u in range(2)]
        xc_in = [sem(f"xc_in{u}") for u in range(2)]
        bn_done, mv_done, ve_done, seeded = sem("bn_done"), sem("mv_done"), sem("ve_done"), sem("seeded")
        bn_seen = sem("bn_seen")
        newton_step, rstd_done = sem("newton_step"), sem("rstd_done")
        norm_done, t_done, hi_done, lo_done = sem("norm_done"), sem("t_done"), sem("hi_done"), sem("lo_done")
        q_done, k_done, v_done = sem("q_done"), sem("k_done"), sem("v_done")
        qk_stored, v_staged = sem("qk_stored"), sem("v_staged")
        v_out = [sem(f"v_out{u}") for u in range(2)]
        v_in = [sem(f"v_in{u}") for u in range(2)]
        chunk_ready, scores_done, probs_done = sem("chunk_ready"), sem("scores_done"), sem("probs_done")
        pv_done, o_taken = sem("pv_done"), sem("o_taken")
        xb_done, ret_hi, ret_lo, proj_done = sem("xb_done"), sem("ret_hi"), sem("ret_lo"), sem("proj_done")
        mid_done, base_done = sem("mid_done"), sem("base_done")
        up_done, gelu_done, act_hi, act_lo = sem("up_done"), sem("gelu_done"), sem("act_hi"), sem("act_lo")
        down_done, final_done = sem("down_done"), sem("final_done")
        y_out = [sem(f"y_out{u}") for u in range(2)]

        def strip_no(b, s):
            return b * STRIPS + index(s)

        def ln_no(b, phase, s):
            return b * 2 * STRIPS + phase * STRIPS + index(s)

        def chunk_no(b, m, c):
            return b * CHUNKS_IMG + m * CHUNKS + index(c)

        def landed(b, s):
            return (b * ((STRIPS + 1 - s[1]) // 2) + s[0] + 1) * 16

        def all_landed(b, par):
            return (b + 1) * ((STRIPS + 1 - par) // 2) * 16

        x_tok = x.rearrange("b h w c -> (b h w) c").rearrange("(s t p) c -> s p t c", t=T, p=P)
        y_tok = out.rearrange("b h w c -> (b h w) c").rearrange("(s t p) c -> s p t c", t=T, p=P)
        v_tok = v_rows.rearrange("b h w c -> (b h w) c").rearrange("(s t p) c -> s p t c", t=T, p=P)

        def dram_strip(view, b, s):
            return view[ds(strip_no(b, s), 1)].rearrange("s p t c -> p (s t) c")

        def tokens(img, s):
            return img[:, :, ds(index(s) * STRIP, STRIP)]

        def lines(img, g, d, c):
            if d:
                return img[:, g, ds(index(c) * CH, CH)].rearrange("p (l n) -> p l n", l=LINES)
            return img[:, g].rearrange("p (h w) -> p w h", w=W)[:, ds(index(c) * LINES, LINES)]

        raw_q = q_img[:, :, :].rearrange("p k n -> p (k n)")
        at = [0]

        def staging(rows, n):
            at[0] += n
            return raw_q[:rows, at[0] - n:at[0]]

        raw_qkv = staging(P, KC * 3 * C).rearrange("p (k n) -> p k n", k=KC)
        raw_proj = staging(P, KC * C).rearrange("p (k n) -> p k n", k=KC)
        raw_up = staging(P, KC * FF).rearrange("p (k n) -> p k n", k=KC)
        raw_down = staging(P, KF * C).rearrange("p (k n) -> p k n", k=KF)
        raw_decay = staging(H, 2 * HEADS * H).rearrange("p (d e n) -> p d e n", d=2, e=HEADS)
        proj_scaled = staging(P, KC * C).rearrange("p (k n) -> p k n", k=KC)
        gamma_row = staging(P, C)
        ln1_b_cols = staging(P, KC * P).rearrange("p (k n) -> p k n", k=KC)
        g1, b1, g2, b2 = (staging(P, KC) for _ in range(4))
        raw_qk_bias, raw_up_bias = staging(P, 2 * KC), staging(P, KF)

        block = ctx.enter_context(nc.Block())

        @block.sync
        def _(sp):
            def by_chunk(v, k):
                return v.rearrange("(k p) -> p k", k=k)

            for dst, src in ((raw_qkv, qkv_w.rearrange("(k p) n -> p k n", p=P)),
                             (raw_proj, proj_w.rearrange("(k p) n -> p k n", p=P)),
                             (raw_up, ffn_w1.rearrange("(k p) n -> p k n", p=P)),
                             (raw_down, ffn_w2.rearrange("(k p) n -> p k n", p=P)),
                             (g1, by_chunk(ln1_g, KC)), (b1, by_chunk(ln1_b, KC)),
                             (g2, by_chunk(ln2_g, KC)), (b2, by_chunk(ln2_b, KC)),
                             (raw_qk_bias, by_chunk(qkv_b[0:2 * C], 2 * KC)),
                             (raw_up_bias, by_chunk(ffn_b1, KF)),
                             (v_bias[:, :], qkv_b[2 * C:3 * C].partition_broadcast(P)),
                             (proj_bias[:, :], proj_b.partition_broadcast(P)),
                             (down_bias[:, :], ffn_b2.partition_broadcast(P)),
                             (gamma_row, gamma.partition_broadcast(P))):
                sp.dma_start(dst, src, allow_slow_non_contiguous=True).then_inc(w_in, 16)
            for d, src in enumerate((decay_h, decay_w)):
                sp.dma_start(raw_decay[:, d], src.rearrange("e q k -> q e k")).then_inc(dw_in, 16)

            with sp.Fori(0, B) as b:
                def first_pass(s, inside):
                    if inside(4):
                        if inside(2):
                            sp.wait_ge(norm_done, ln_no(b, 0, shifted(s, 2)) + 1)
                        u = shifted(s, 4)
                        sp.dma_start(x_in[:, u[1]], dram_strip(x_tok, b, u)).then_inc(xa_in[u[1]], 16)
                    if inside(0):
                        sp.wait_ge(v_staged, strip_no(b, s) + 1)
                        sp.dma_start(dram_strip(v_tok, b, s), stage[:, s[1]]).then_inc(v_out[s[1]], 16)

                run_slots(sp, first_pass, STRIPS, 0, 4)

                for u in range(2):
                    sp.wait_ge(v_out[u], all_landed(b, u))
                for m, (g, d) in enumerate(COMBOS):
                    v_img = v_rows[ds(b, 1), :, :, g * P:(g + 1) * P].rearrange("b h w c -> (b h) w c")

                    def load_v(c, inside, m=m, d=d, v_img=v_img):
                        if inside(0):
                            if m or inside(-2):
                                sp.wait_ge(pv_done, (chunk_no(b, m, c) - 1) * LINES)
                            src = v_img[ds(index(c) * LINES, LINES)].rearrange("l p c -> p l c") if d \
                                else v_img[:, ds(index(c) * LINES, LINES)]
                            sp.dma_start(v_chunk[:, c[1]], src).then_inc(v_in[c[1]], 16)

                    run_slots(sp, load_v, CHUNKS, 2, 0)

                sp.wait_ge(o_taken, (b + 1) * CHUNKS_IMG)

                def second_pass(s, inside):
                    if inside(2):
                        if inside(0):
                            sp.wait_ge(mid_done, strip_no(b, s) + 1)
                        u = shifted(s, 2)
                        sp.dma_start(x_in[:, u[1]], dram_strip(x_tok, b, u)).then_inc(xc_in[u[1]], 16)
                    if inside(-2):
                        u = shifted(s, -2)
                        sp.wait_ge(final_done, strip_no(b, u) + 1)
                        sp.dma_start(dram_strip(y_tok, b, u), stage[:, u[1]]).then_inc(y_out[u[1]], 16)

                run_slots(sp, second_pass, STRIPS, 2, 2)
            for u in range(2):
                sp.wait_ge(y_out[u], all_landed(B - 1, u))

        @block.gpsimd
        def _(pool):
            pool.memset(three_halves[:, :], 1.5)
            pool.memset(ident[:, :], 0.0).then_inc(ident_clear, 1)
            pool.wait_ge(ident_clear, 1)
            pool.affine_select(out=ident[:, :], in_=ident[:, :], compare_op=ALU.not_equal, fill=1.0,
                               base=0, pattern=[[-1, P]], channel_multiplier=1).then_inc(ident_done, 1)

            def rsqrt(n, par):
                pool.wait_ge(seeded, 2 * n + 2)
                y, t = rstd[:, par], newton[:, par]
                steps = 4 * NEWTON_STEPS
                done = 0
                for step in range(NEWTON_STEPS):
                    for ins in (lambda: pool.tensor_tensor(t, y, y, ALU.mult),
                                lambda: pool.tensor_tensor(t, t, neg_half[:, par], ALU.mult),
                                lambda: pool.tensor_tensor(t, t, three_halves[:, :], ALU.add),
                                lambda: pool.tensor_tensor(y, y, t, ALU.mult)):
                        done += 1
                        if done < steps:
                            ins().then_inc(newton_step, 1)
                            pool.wait_ge(newton_step, n * (steps - 1) + done)
                        else:
                            ins().then_inc(rstd_done, 1)

            pool.wait_ge(setup_ready, 1)
            with pool.Fori(0, B) as b:
                run_slots(pool, lambda s, inside: rsqrt(ln_no(b, 0, s), s[1]), STRIPS, 0, 0)

                def second_pass(s, inside):
                    if inside(1):
                        u = shifted(s, 1)
                        pool.wait_ge(xc_in[u[1]], landed(b, u))
                        pool.tensor_tensor(x_in[:, u[1]], x_in[:, u[1]],
                                           proj_bias[:, :].unsqueeze(1).broadcast_to([P, T, C]),
                                           ALU.add).then_inc(xb_done, 1)
                    if inside(0):
                        rsqrt(ln_no(b, 1, s), s[1])
                        pool.wait_ge(mid_done, strip_no(b, s) + 1)
                        if inside(-2):
                            pool.wait_ge(y_out[s[1]], landed(b, s) - 16)
                        pool.tensor_tensor(stage[:, s[1]], x_mid[:, s[1]],
                                           down_bias[:, :].unsqueeze(1).broadcast_to([P, T, C]),
                                           ALU.add).then_inc(base_done, 1)

                run_slots(pool, second_pass, STRIPS, 2, 1)

        @block.tensor
        def _(pe):
            pe.wait_ge(ident_done, 1)
            pe.wait_ge(dw_in, 32)
            for d in range(2):
                for g in range(KC):
                    for j in range(HG):
                        last = pe.transpose(bank[2 * d + g][:H, j * H:(j + 1) * H],
                                            raw_decay[:, d, g * HG + j, :], ident[:H, :H])
            last.then_inc(setup_pe, 1)
            pe.wait_ge(setup_v, 1)
            for n, w, vec in [(n, raw_qkv, b1) for n in range(2 * KC)] + [(n, raw_up, b2) for n in range(KF)]:
                o = n if w is raw_qkv else 2 * KC + n
                for k in range(KC):
                    pe.matmul(bank[4][:, o:o + 1], w[:, k, n * P:(n + 1) * P], vec[:, k:k + 1],
                              start=(k == 0), stop=(k == KC - 1))
            for k in range(KC):
                last = pe.matmul(bank[5][:, 0:C], ln1_b_cols[:, k, :], raw_qkv[:, k, 2 * C:3 * C],
                                 start=(k == 0), stop=(k == KC - 1))
            last.then_inc(setup_pe, 1)
            pe.wait_ge(setup_ready, 1)

            def transposes(n, par):
                pe.wait_ge(norm_done, n + 1)
                for k in range(KC):
                    for t in range(T):
                        last = pe.transpose(t_bank[par][:, k * STRIP + t * P:k * STRIP + (t + 1) * P],
                                            x_norm[:, par, t, k * P:(k + 1) * P], ident[:, :])
                last.then_inc(t_done, 1)

            def split_product(o, left, right, chunks):
                terms = [(k, a, c) for k in range(chunks) for a, c in ((0, 0), (0, 1), (1, 0))]
                for i, (k, a, c) in enumerate(terms):
                    last = pe.matmul(o, left(a, k), right(c, k), start=(i == 0), stop=(i == len(terms) - 1))
                return last

            with pe.Fori(0, B) as b:
                def first_pass(s, inside):
                    if inside(1):
                        u = shifted(s, 1)
                        transposes(ln_no(b, 0, u), u[1])
                    if inside(0):
                        pe.wait_ge(lo_done, ln_no(b, 0, s) + 1)
                        if inside(-2):
                            pe.wait_ge(qk_stored, strip_no(b, s) - 1)
                            pe.wait_ge(v_staged, strip_no(b, s) - 1)
                        h = h_t[:, s[1]]
                        for dst, col, signal in ((q_bank, 0, q_done), (k_bank, C, k_done)):
                            for g in range(KC):
                                n = col + g * P
                                last = split_product(dst[s[1]][:, g * STRIP:(g + 1) * STRIP],
                                                     lambda a, k: w_qkv[:, a, k, n:n + P],
                                                     lambda c, k: h[:, c, k, :], KC)
                            last.then_inc(signal, 1)
                        for t in range(T):
                            last = split_product(v_bank[s[1]][:, t * C:(t + 1) * C],
                                                 lambda a, k: h[:, a, k, t * P:(t + 1) * P],
                                                 lambda c, k: w_qkv[:, c, k, 2 * C:3 * C], KC)
                        last.then_inc(v_done, 1)

                run_slots(pe, first_pass, STRIPS, 2, 1)

                pe.wait_ge(qk_stored, (b + 1) * STRIPS)
                pe.wait_ge(v_staged, (b + 1) * STRIPS)
                PAIR = 2 * LINES

                def scores(half, j):
                    c, l = (half + j // PAIR, j % PAIR // LINES), j % LINES
                    if l == 0:
                        pe.wait_ge(chunk_ready, b * CHUNKS_IMG + index(c) + 1)
                    pe.matmul(s_bank[l][:H, 0:HG * H], k_chunk[:, c[1], l * H:(l + 1) * H],
                              q_blocks[:, c[1], :, l * H:(l + 1) * H],
                              start=True, stop=True).then_inc(scores_done, 1)

                def values(half, j, first):
                    c, l = (half, j // LINES), j % LINES
                    n = b * CHUNKS_IMG + index(c)
                    if l == 0:
                        pe.wait_ge(v_in[c[1]], (b * (CHUNKS_IMG // 2) + half + 1) * 16)
                        if not first:
                            pe.wait_ge(o_taken, n - 1)
                    pe.wait_ge(probs_done, n * LINES + l + 1)
                    for e in range(HG):
                        last = pe.matmul(o_bank[c[1]][e * HD:(e + 1) * HD, l * H:(l + 1) * H],
                                         v_chunk[:, c[1], l, e * HD:(e + 1) * HD],
                                         probs[:, l, e * H:(e + 1) * H], start=True, stop=True,
                                         skip_group_check=True)
                    last.then_inc(pv_done, 1)

                LEAD = 2

                def pair(half, first=False, final=False):
                    for j in range(PAIR):
                        if not final or j + LEAD < PAIR:
                            scores(half, j + LEAD)
                        values(half, j, first)

                for j in range(LEAD):
                    scores(0, j)
                pair(0, first=True)
                with pe.Fori(1, CHUNKS_IMG // 2 - 1) as half:
                    pair(half)
                pair(CHUNKS_IMG // 2 - 1, final=True)

                pe.wait_ge(o_taken, (b + 1) * CHUNKS_IMG)

                def second_pass(s, inside):
                    if inside(0):
                        pe.wait_ge(ret_lo, strip_no(b, s) + 1)
                        for t in range(T):
                            last = split_product(proj_bank[s[1]][:, t * C:(t + 1) * C],
                                                 lambda a, k: ret_t[:, a, k, t * P:(t + 1) * P],
                                                 lambda c, k: w_proj[:, c, k, :], KC)
                        last.then_inc(proj_done, 1)
                    if inside(-1):
                        u = shifted(s, -1)
                        transposes(ln_no(b, 1, u), u[1])
                    if inside(-2):
                        u = shifted(s, -2)
                        pe.wait_ge(act_lo, strip_no(b, u) + 1)
                        if inside(-4):
                            pe.wait_ge(final_done, strip_no(b, u) - 1)
                        for t in range(T):
                            last = split_product(down_bank[u[1]][:, t * C:(t + 1) * C],
                                                 lambda a, k: act_t[:, a, k, t * P:(t + 1) * P],
                                                 lambda c, k: w_down[:, c, k, :], KF)
                        last.then_inc(down_done, 1)
                    if inside(-1):
                        u = shifted(s, -1)
                        pe.wait_ge(lo_done, ln_no(b, 1, u) + 1)
                        for n in range(KF):
                            last = split_product(up_bank[n // 2][:, n % 2 * STRIP:(n % 2 + 1) * STRIP],
                                                 lambda a, k: w_up[:, a, k, n * P:(n + 1) * P],
                                                 lambda c, k: h_t[:, u[1], c, k, :], KC)
                            if n % 2:
                                last.then_inc(up_done, 1)

                run_slots(pe, second_pass, STRIPS, 4, 0)
                pe.wait_ge(final_done, (b + 1) * STRIPS)

        @block.scalar
        def _(act):
            act.wait_ge(setup_ready, 1)

            def high_part(n, par):
                act.wait_ge(t_done, n + 1)
                act.activation(h_t[:, par, 0], t_bank[par][:, :].rearrange("p (k n) -> p k n", k=KC),
                               ACT.Copy).then_inc(hi_done, 1)

            with act.Fori(0, B) as b:
                def first_pass(s, inside):
                    if inside(1):
                        u = shifted(s, 1)
                        high_part(ln_no(b, 0, u), u[1])
                    if inside(0):
                        for img, src, signal, o in ((q_img, q_bank, q_done, 0), (k_img, k_bank, k_done, KC)):
                            act.wait_ge(signal, strip_no(b, s) + 1)
                            for g in range(KC):
                                last = act.activation(img[:, g, ds(index(s) * STRIP, STRIP)],
                                                      src[s[1]][:, g * STRIP:(g + 1) * STRIP],
                                                      ACT.Identity, bias=qk_bias[:, o + g:o + g + 1])
                        last.then_inc(qk_stored, 1)

                run_slots(act, first_pass, STRIPS, 0, 1)

                act.wait_ge(qk_stored, (b + 1) * STRIPS)

                def prepare(m, c, first=False):
                    g, d = COMBOS[m]
                    if not first:
                        act.wait_ge(scores_done, (chunk_no(b, m, c) - 1) * LINES)
                    act.activation(k_chunk[:, c[1]].rearrange("p (l n) -> p l n", l=LINES),
                                   lines(k_img, g, d, c), ACT.Copy)
                    for e in range(HG):
                        rows = slice(e * HD, (e + 1) * HD)
                        last = act.activation(q_blocks[rows, c[1], e].rearrange("p (l n) -> p l n", l=LINES),
                                              lines(q_img, g, d, c)[rows], ACT.Copy)
                    last.then_inc(chunk_ready, 1)

                def store_columns(m, c):
                    act.wait_ge(pv_done, (chunk_no(b, m, c) + 1) * LINES)
                    act.activation(out_h[:, :].rearrange("p (h w) -> p w h", w=W)[:, ds(index(c) * LINES, LINES)],
                                   o_bank[c[1]][:, 0:CH].rearrange("p (l n) -> p l n", l=LINES),
                                   ACT.Copy).then_inc(o_taken, 1)

                prepare(0, (0, 0), first=True)
                for m, (g, d) in enumerate(COMBOS):
                    if d == 0 and m:
                        act.wait_ge(o_taken, b * CHUNKS_IMG + m * CHUNKS)

                    def slot(c, inside, m=m, d=d):
                        if inside(1) and inside(0):
                            prepare(m, shifted(c, 1), first=(m == 0 and not inside(-1)))
                        elif inside(0) and m + 1 < len(COMBOS):
                            prepare(m + 1, (0, 0))
                        if inside(-1) and d == 0:
                            store_columns(m, shifted(c, -1))

                    run_slots(act, slot, CHUNKS, 1, 1)

                act.wait_ge(o_taken, (b + 1) * CHUNKS_IMG)

                def second_pass(s, inside):
                    if inside(-1):
                        u = shifted(s, -1)
                        high_part(ln_no(b, 1, u), u[1])
                    if inside(1):
                        u = shifted(s, 1)
                        if inside(0):
                            act.wait_ge(proj_done, strip_no(b, u))
                        act.activation(ret_t[:, 0], tokens(q_img, u), ACT.Copy).then_inc(ret_hi, 1)
                    if inside(-1):
                        n = strip_no(b, u := shifted(s, -1))
                        for k in range(KF):
                            if k % 2 == 0:
                                act.wait_ge(up_done, n * (KF // 2) + k // 2 + 1)
                            last = act.activation(act_f[:, k], up_bank[k // 2][:, k % 2 * STRIP:(k % 2 + 1) * STRIP],
                                                  ACT.Gelu, bias=up_bias[:, k:k + 1])
                        last.then_inc(gelu_done, 1)
                        act.wait_ge(gelu_done, n + 1)
                        act.activation(act_t[:, 0], act_f, ACT.Copy).then_inc(act_hi, 1)

                run_slots(act, second_pass, STRIPS, 1, 1)

        @block.vector
        def _(dve):
            links = [0]

            def link(ins):
                links[0] += 1
                ins.then_inc(setup_link, 1)
                dve.wait_ge(setup_link, links[0])

            dve.memset(q_blocks[:, :, :, :], 0.0)
            dve.wait_ge(ident_done, 1)
            dve.wait_ge(w_in, 14 * 16)
            for k in range(KC):
                last = dve.tensor_scalar(ln1_b_cols[:, k, :], ident[:, :], 0.0, b1[:, k:k + 1], ALU.mult, ALU.add)
            last.then_inc(setup_v, 1)
            for raw, w, gain in ((raw_qkv, w_qkv, g1), (raw_up, w_up, g2)):
                for k in range(KC):
                    link(dve.tensor_scalar(w[:, 0, k], raw[:, k], gain[:, k:k + 1], None, ALU.mult))
                    dve.scalar_tensor_tensor(out=w[:, 1, k], in0=raw[:, k], scalar=gain[:, k:k + 1],
                                             in1=w[:, 0, k].bitcast(F32), op0=ALU.mult, op1=ALU.subtract)
            link(dve.tensor_tensor(proj_scaled, raw_proj, gamma_row.unsqueeze(1).broadcast_to([P, KC, C]), ALU.mult))
            for raw, w in ((proj_scaled, w_proj), (raw_down, w_down)):
                link(dve.tensor_copy(w[:, 0], raw))
                dve.tensor_tensor(w[:, 1], raw, w[:, 0].bitcast(F32), ALU.subtract)
            dve.tensor_tensor(proj_bias[:, :], proj_bias[:, :], gamma_row, ALU.mult)
            dve.wait_ge(setup_pe, 1)
            for d in range(2):
                for g in range(KC):
                    dve.tensor_scalar(decay[:, d, g], bank[2 * d + g][:H, 0:HG * H], 0.5, None, ALU.mult)
            dve.wait_ge(setup_pe, 2)
            dve.tensor_tensor(qk_bias[:, :], bank[4][:, 0:2 * KC], raw_qk_bias, ALU.add)
            dve.tensor_tensor(up_bias[:, :], bank[4][:, 2 * KC:2 * KC + KF], raw_up_bias, ALU.add)
            dve.tensor_tensor(v_bias[:, :], bank[5][:, 0:C], v_bias[:, :], ALU.add).then_inc(setup_ready, 1)
            dve.wait_ge(setup_ready, 1)

            def statistics(n, par, src):
                for t in range(T):
                    dve.bn_stats(bn[:, par, t], src[:, t]).then_inc(bn_done, 1)
                dve.wait_ge(bn_done, (n + 1) * T)
                dve.sem_inc(bn_seen, 1)
                for t in range(T):
                    dve.bn_aggr(mean_var[:, par, t], bn[:, par, t]).then_inc(mv_done, 1)
                dve.wait_ge(mv_done, (n + 1) * T)
                dve.tensor_scalar(var_eps[:, par], mean_var[:, par, :, 1], EPS, None, ALU.add).then_inc(ve_done, 1)
                dve.tensor_scalar(neg_half[:, par], mean_var[:, par, :, 1], EPS, -0.5, ALU.add,
                                  ALU.mult).then_inc(seeded, 1)
                dve.wait_ge(ve_done, n + 1)
                dve.tensor_scalar(rstd[:, par].bitcast(I32), var_eps[:, par].bitcast(I32), -0.5, RSQRT_SEED,
                                  ALU.mult, ALU.add).then_inc(seeded, 1)

            def normalise(n, par, src):
                dve.wait_ge(rstd_done, n + 1)
                for t in range(T):
                    last = dve.tensor_scalar(x_norm[:, par, t], src[:, t], mean_var[:, par, t, 0:1],
                                             rstd[:, par, t:t + 1], ALU.subtract, ALU.mult)
                last.then_inc(norm_done, 1)

            def low_part(n, par):
                dve.wait_ge(hi_done, n + 1)
                dve.tensor_tensor(h_t[:, par, 1], t_bank[par][:, :].rearrange("p (k n) -> p k n", k=KC),
                                  h_t[:, par, 0].bitcast(F32), ALU.subtract).then_inc(lo_done, 1)

            with dve.Fori(0, B) as b:
                def first_pass(s, inside):
                    if inside(1):
                        u = shifted(s, 1)
                        low_part(ln_no(b, 0, u), u[1])
                    if inside(2):
                        u = shifted(s, 2)
                        normalise(ln_no(b, 0, u), u[1], x_in[:, u[1]])
                    if inside(3):
                        u = shifted(s, 3)
                        dve.wait_ge(xa_in[u[1]], landed(b, u))
                        statistics(ln_no(b, 0, u), u[1], x_in[:, u[1]])
                    if inside(0):
                        dve.wait_ge(v_done, strip_no(b, s) + 1)
                        if inside(-2):
                            dve.wait_ge(v_out[s[1]], landed(b, s) - 16)
                        dve.tensor_tensor(stage[:, s[1]], v_bank[s[1]][:, :].rearrange("p (t c) -> p t c", t=T),
                                          v_bias[:, :].unsqueeze(1).broadcast_to([P, T, C]),
                                          ALU.add).then_inc(v_staged, 1)

                run_slots(dve, first_pass, STRIPS, 2, 3)

                def store_rows(m, c):
                    g = COMBOS[m][0]
                    dve.wait_ge(pv_done, (chunk_no(b, m, c) + 1) * LINES)
                    span = ds(index(c) * CH, CH)
                    dve.tensor_tensor(q_img[:, g, span], o_bank[c[1]][:, 0:CH], out_h[:, span],
                                      ALU.add).then_inc(o_taken, 1)

                for m, (g, d) in enumerate(COMBOS):
                    def slot(c, inside, m=m, g=g, d=d):
                        if not inside(0):
                            return
                        n = chunk_no(b, m, c)
                        for l in range(LINES):
                            if l == LINES // 2:
                                if inside(-1) and d == 1:
                                    if not inside(-2):
                                        dve.wait_ge(o_taken, b * CHUNKS_IMG + m * CHUNKS)
                                    store_rows(m, shifted(c, -1))
                                elif not inside(-1) and m and d == 0:
                                    store_rows(m - 1, ((CHUNKS - 1) // 2, (CHUNKS - 1) % 2))
                            dve.wait_ge(scores_done, n * LINES + l + 1)
                            if m or inside(-1):
                                dve.wait_ge(pv_done, n * LINES + l + 1 - LINES)
                            dve.tensor_tensor(probs[:, l], s_bank[l][:H, 0:HG * H], decay[:, d, g],
                                              ALU.mult).then_inc(probs_done, 1)

                    run_slots(dve, slot, CHUNKS, 2, 0)
                store_rows(len(COMBOS) - 1, ((CHUNKS - 1) // 2, (CHUNKS - 1) % 2))
                dve.wait_ge(o_taken, (b + 1) * CHUNKS_IMG)

                def second_pass(s, inside):
                    if inside(0):
                        n = strip_no(b, s)
                        dve.wait_ge(proj_done, n + 1)
                        dve.wait_ge(xb_done, n + 1)
                        if inside(-2):
                            dve.wait_ge(base_done, n - 1)
                        dve.tensor_tensor(x_mid[:, s[1]], proj_bank[s[1]][:, :].rearrange("p (t c) -> p t c", t=T),
                                          x_in[:, s[1]], ALU.add).then_inc(mid_done, 1)
                        dve.wait_ge(mid_done, n + 1)
                        statistics(ln_no(b, 1, s), s[1], x_mid[:, s[1]])
                    if inside(-1):
                        u = shifted(s, -1)
                        low_part(ln_no(b, 1, u), u[1])
                    if inside(1):
                        u = shifted(s, 1)
                        dve.wait_ge(ret_hi, strip_no(b, u) + 1)
                        dve.tensor_tensor(ret_t[:, 1], tokens(q_img, u), ret_t[:, 0].bitcast(F32),
                                          ALU.subtract).then_inc(ret_lo, 1)
                    if inside(0):
                        normalise(ln_no(b, 1, s), s[1], x_mid[:, s[1]])
                    if inside(-2):
                        u = shifted(s, -2)
                        dve.wait_ge(down_done, strip_no(b, u) + 1)
                        dve.wait_ge(base_done, strip_no(b, u) + 1)
                        dve.tensor_tensor(stage[:, u[1]], down_bank[u[1]][:, :].rearrange("p (t c) -> p t c", t=T),
                                          stage[:, u[1]], ALU.add).then_inc(final_done, 1)
                    if inside(-1):
                        n = strip_no(b, shifted(s, -1))
                        dve.wait_ge(act_hi, n + 1)
                        dve.tensor_tensor(act_t[:, 1], act_f, act_t[:, 0].bitcast(F32),
                                          ALU.subtract).then_inc(act_lo, 1)

                run_slots(dve, second_pass, STRIPS, 2, 1)
                for u in range(2):
                    dve.wait_ge(y_out[u], all_landed(b, u))


NAMES = ("x", "L0_conv_decay_h", "L0_conv_decay_w", "L0_conv_qkv_w", "L0_conv_qkv_b", "L0_conv_proj_w",
         "L0_conv_proj_b", "L0_conv_ln1_g", "L0_conv_ln1_b", "L0_conv_ln2_g", "L0_conv_ln2_b",
         "L0_conv_ffn_w1", "L0_conv_ffn_b1", "L0_conv_ffn_w2", "L0_conv_ffn_b2", "L0_conv_gamma")


def kernel(**inputs):
    import numpy as np
    import concourse.bacc as bacc
    from concourse.bass_utils import run_bass_kernel_spmd

    nc = bacc.Bacc("TRN2", target_bir_lowering=False, num_devices=1)
    arrays, args = {}, []
    for name in NAMES:
        a = np.ascontiguousarray(inputs[name])
        arrays[f"in_{name}"] = a
        args.append(nc.dram_tensor(f"in_{name}", a.shape, F32, kind="ExternalInput").ap())
    shape = inputs["x"].shape
    v_rows = nc.dram_tensor("v_rows", shape, F32, kind="Internal").ap()
    out = nc.dram_tensor("out", shape, F32, kind="ExternalOutput").ap()
    build(nc, *args, v_rows, out)
    result = run_bass_kernel_spmd(nc, [arrays], core_ids=[0])
    return result.results[0]["out"]
```

```python
from contextlib import ExitStack

import concourse.bass as bass
from concourse import mybir

ALU = mybir.AluOpType
ACT = mybir.ActivationFunctionType
F32 = mybir.dt.float32
F32R = mybir.dt.float32r
I32 = mybir.dt.int32
ds = bass.ds

P = 128
HEADS = 8
EPS = 1e-5
RSQRT_SEED = float(0x5F3759DF)
NEWTON_STEPS = 3


def shifted(unit, k):
    half, par = unit
    return half + (par + k) // 2, (par + k) % 2


def index(unit):
    return 2 * unit[0] + unit[1]


def one_slot(slot, s, count):
    slot((s // 2, s % 2), lambda k: 0 <= s + k < count)


def run_slots(eng, slot, count, back, ahead, start=None, stop=None):
    start = -ahead if start is None else start
    stop = count + back if stop is None else stop
    first = max(back + back % 2, start + start % 2)
    last = (count - ahead) // 2 * 2
    for s in range(start, first):
        one_slot(slot, s, count)
    with eng.Fori(first // 2, last // 2) as half:
        for par in range(2):
            slot((half, par), lambda k: True)
    for s in range(last, stop):
        one_slot(slot, s, count)


def run_images(eng, image, images):
    with eng.Fori(0, images - 1) as b:
        image(b, True)
    image(images - 1, False)


def build(nc, x, decay_h, decay_w, qkv_w, qkv_b, proj_w, proj_b, ln1_g, ln1_b, ln2_g, ln2_b,
          ffn_w1, ffn_b1, ffn_w2, ffn_b2, gamma, v_rows, out):
    B, H, W, C = x.shape
    assert H == W and C == 2 * P and H % 8 == 0
    N = H * W
    KC = C // P
    HD = C // HEADS
    HG = HEADS // KC
    FF = ffn_w1.shape[1]
    KF = FF // P
    T = 2
    STRIP = T * P
    STRIPS = N // STRIP
    LINES = 4
    CH = LINES * W
    CHUNKS = H // LINES
    ROWS, COLS = 1, 0
    COMBOS = [(g, d) for g in range(KC) for d in (ROWS, COLS)]
    CHUNKS_IMG = len(COMBOS) * CHUNKS
    assert N % STRIP == 0 and CHUNKS % 2 == 0 and HD == 32

    with ExitStack() as ctx:
        def sb(name, shape, dt=F32):
            return ctx.enter_context(nc.sbuf_tensor(name, shape, dt))

        def sem(name):
            return ctx.enter_context(nc.semaphore(name))

        img = sb("img", [P, 3 * KC - 1, N])
        ret, q_img, k_img = img[:, 0:KC], img[:, KC - 1:2 * KC - 1], img[:, 2 * KC - 1:3 * KC - 1]

        def strip_buffers(region, n):
            w = 2 * T * C
            return [region[:, i * w:(i + 1) * w].rearrange("p (u t c) -> p u t c", u=2, t=T) for i in range(n)]

        x_first, norm_first, v_stage = strip_buffers(img[:, 0], 3)
        x_second, norm_second, x_mid, y_stage = strip_buffers(k_img[:, 0], 4)
        act_f = k_img[:, 0, 8 * T * C:8 * T * C + KF * STRIP].rearrange("p (k n) -> p k n", k=KF)
        w_qkv = sb("w_qkv", [P, 2, KC, 3 * C], F32R)
        w_proj = sb("w_proj", [P, 2, KC, C], F32R)
        w_up = sb("w_up", [P, 2, KC, FF], F32R)
        w_down = sb("w_down", [P, 2, KF, C], F32R)
        h_t = sb("h_t", [P, 2, 2, KC, STRIP], F32R)
        ret_t = sb("ret_t", [P, 2, KC, STRIP], F32R)
        act_t = sb("act_t", [P, 2, KF, STRIP], F32R)
        decay = sb("decay", [H, 2, KC, HG * H])
        ident = sb("ident", [P, P])
        v_bias = sb("v_bias", [P, C])
        proj_bias = sb("proj_bias", [P, C])
        down_bias = sb("down_bias", [P, C])
        qk_bias = sb("qk_bias", [P, 2 * KC])
        up_bias = sb("up_bias", [P, KF])
        q_blocks = sb("q_blocks", [P, 2, HG, CH])
        k_chunk = sb("k_chunk", [P, 2, CH])
        v_chunk = sb("v_chunk", [H, 2, LINES, P])
        probs = sb("probs", [H, LINES, HG * H])
        bn = sb("bn", [P, 2, T, 6])
        mean_var = sb("mean_var", [P, 2, T, 2])
        var_eps = sb("var_eps", [P, 2, T])
        neg_half = sb("neg_half", [P, 2, T])
        rstd = sb("rstd", [P, 2, T])
        newton = sb("newton", [P, 2, T])
        shift = sb("shift", [P, 2, T])

        bank = [ctx.enter_context(nc.psum_tensor(f"bank{i}", [P, 512], F32)) for i in range(8)]
        t_bank = bank[0:2]
        q_bank, k_bank, v_bank = (bank[2], bank[4]), (bank[3], bank[5]), bank[6:8]
        proj_bank, up_bank, down_bank = bank[6:8], bank[2:4], bank[4:6]
        s_bank, o_bank = bank[0:4], bank[4:6]

        w_in, dw_in = sem("w_in"), sem("dw_in")
        ident_clear, ident_done = sem("ident_clear"), sem("ident_done")
        setup_v, setup_pe, setup_ready = sem("setup_v"), sem("setup_pe"), sem("setup_ready")
        setup_link = sem("setup_link")
        xa_in = [sem(f"xa_in{u}") for u in range(2)]
        xc_in = [sem(f"xc_in{u}") for u in range(2)]
        bn_done, mv_done, ve_done = sem("bn_done"), sem("mv_done"), sem("ve_done")
        bn_seen = sem("bn_seen")
        newton_step, shift_done = sem("newton_step"), sem("shift_done")
        norm1_done, norm2_done, t_done, hi_done, lo_done = sem("norm1_done"), sem("norm2_done"), sem("t_done"), sem("hi_done"), sem("lo_done")
        q_done, k_done, v_done = sem("q_done"), sem("k_done"), sem("v_done")
        qk_stored, v_copied, v_staged = sem("qk_stored"), sem("v_copied"), sem("v_staged")
        v_out = [sem(f"v_out{u}") for u in range(2)]
        v_in = [sem(f"v_in{u}") for u in range(2)]
        chunk_ready, scores_done, probs_done = sem("chunk_ready"), sem("scores_done"), sem("probs_done")
        pv_done, o_taken = sem("pv_done"), sem("o_taken")
        xb_done, ret_hi, ret_lo, proj_done = sem("xb_done"), sem("ret_hi"), sem("ret_lo"), sem("proj_done")
        mid_done, base_done = sem("mid_done"), sem("base_done")
        up_done, gelu_done, act_hi = sem("up_done"), sem("gelu_done"), sem("act_hi")
        act_lo = [sem(f"act_lo{u}") for u in range(2)]
        down_done, final_done = sem("down_done"), sem("final_done")
        y_out = [sem(f"y_out{u}") for u in range(2)]

        def strip_no(b, s):
            return b * STRIPS + index(s)

        def ln_no(b, phase, s):
            return b * 2 * STRIPS + phase * STRIPS + index(s)

        def chunk_no(b, m, c):
            return b * CHUNKS_IMG + m * CHUNKS + index(c)

        def landed(b, s):
            return (b * ((STRIPS + 1 - s[1]) // 2) + s[0] + 1) * 16

        def all_landed(b, par):
            return (b + 1) * ((STRIPS + 1 - par) // 2) * 16

        x_tok = x.rearrange("b h w c -> (b h w) c").rearrange("(s t p) c -> s p t c", t=T, p=P)
        y_tok = out.rearrange("b h w c -> (b h w) c").rearrange("(s t p) c -> s p t c", t=T, p=P)
        v_tok = v_rows.rearrange("b h w c -> (b h w) c").rearrange("(s t p) c -> s p t c", t=T, p=P)

        def dram_strip(view, b, s):
            return view[ds(strip_no(b, s), 1)].rearrange("s p t c -> p (s t) c")

        def tokens(img, s):
            return img[:, :, ds(index(s) * STRIP, STRIP)]

        def lines(img, g, d, c):
            if d:
                return img[:, g, ds(index(c) * CH, CH)].rearrange("p (l n) -> p l n", l=LINES)
            return img[:, g].rearrange("p (h w) -> p w h", w=W)[:, ds(index(c) * LINES, LINES)]

        raw_q = q_img.rearrange("p k n -> p (k n)")
        at = [0]

        def staging(rows, n):
            at[0] += n
            return raw_q[:rows, at[0] - n:at[0]]

        raw_qkv = staging(P, KC * 3 * C).rearrange("p (k n) -> p k n", k=KC)
        raw_proj = staging(P, KC * C).rearrange("p (k n) -> p k n", k=KC)
        raw_up = staging(P, KC * FF).rearrange("p (k n) -> p k n", k=KC)
        raw_down = staging(P, KF * C).rearrange("p (k n) -> p k n", k=KF)
        raw_decay = staging(H, 2 * HEADS * H).rearrange("p (d e n) -> p d e n", d=2, e=HEADS)
        proj_scaled = staging(P, KC * C).rearrange("p (k n) -> p k n", k=KC)
        gamma_row = staging(P, C)
        ln1_b_cols = staging(P, KC * P).rearrange("p (k n) -> p k n", k=KC)
        g1, b1, g2, b2 = (staging(P, KC) for _ in range(4))
        raw_qk_bias, raw_up_bias = staging(P, 2 * KC), staging(P, KF)

        def low_act(eng, b, s, half):
            ks = slice(half * KF // 2, (half + 1) * KF // 2)
            eng.wait_ge(act_hi, 2 * strip_no(b, s) + half + 1)
            eng.tensor_tensor(act_t[:, 1, ks], act_f[:, ks], act_t[:, 0, ks].bitcast(F32),
                              ALU.subtract).then_inc(act_lo[half], 1)

        block = ctx.enter_context(nc.Block())

        @block.sync
        def _(sp):
            def by_chunk(v, k):
                return v.rearrange("(k p) -> p k", k=k)

            for dst, src in ((raw_qkv, qkv_w.rearrange("(k p) n -> p k n", p=P)),
                             (raw_proj, proj_w.rearrange("(k p) n -> p k n", p=P)),
                             (raw_up, ffn_w1.rearrange("(k p) n -> p k n", p=P)),
                             (raw_down, ffn_w2.rearrange("(k p) n -> p k n", p=P)),
                             (g1, by_chunk(ln1_g, KC)), (b1, by_chunk(ln1_b, KC)),
                             (g2, by_chunk(ln2_g, KC)), (b2, by_chunk(ln2_b, KC)),
                             (raw_qk_bias, by_chunk(qkv_b[0:2 * C], 2 * KC)),
                             (raw_up_bias, by_chunk(ffn_b1, KF)),
                             (v_bias[:, :], qkv_b[2 * C:3 * C].partition_broadcast(P)),
                             (proj_bias[:, :], proj_b.partition_broadcast(P)),
                             (down_bias[:, :], ffn_b2.partition_broadcast(P)),
                             (gamma_row, gamma.partition_broadcast(P))):
                sp.dma_start(dst, src, allow_slow_non_contiguous=True).then_inc(w_in, 16)
            for d, src in enumerate((decay_h, decay_w)):
                sp.dma_start(raw_decay[:, d], src.rearrange("e q k -> q e k")).then_inc(dw_in, 16)

            def load_first(b, s, inside):
                if inside(2):
                    sp.wait_ge(norm1_done, strip_no(b, shifted(s, 2)) + 1)
                u = shifted(s, 4)
                sp.dma_start(x_first[:, u[1]], dram_strip(x_tok, b, u)).then_inc(xa_in[u[1]], 16)

            def image(b, more):
                def load_v(m, c):
                    g, d = COMBOS[m]
                    v_img = v_rows[ds(b, 1), :, :, g * P:(g + 1) * P].rearrange("b h w c -> (b h) w c")
                    span = ds(index(c) * LINES, LINES)
                    src = v_img[span].rearrange("l p c -> p l c") if d == ROWS else v_img[:, span]
                    sp.dma_start(v_chunk[:, c[1]], src).then_inc(v_in[c[1]], 16)

                def stage_v(s, inside):
                    if inside(4):
                        load_first(b, s, inside)
                    if inside(0) and not inside(1):
                        sp.wait_ge(v_out[0], landed(b, (1, 0)))
                        sp.wait_ge(v_out[1], landed(b, (0, 1)))
                        for c in range(2):
                            load_v(0, (0, c))
                    if inside(0):
                        sp.wait_ge(v_staged, strip_no(b, s) + 1)
                        sp.dma_start(dram_strip(v_tok, b, s), v_stage[:, s[1]]).then_inc(v_out[s[1]], 16)

                run_slots(sp, stage_v, STRIPS, 0, 4, start=0)

                for u in range(2):
                    sp.wait_ge(v_out[u], all_landed(b, u))
                for m in range(len(COMBOS)):
                    def slot(c, inside, m=m):
                        if inside(0) and (m or inside(-2)):
                            sp.wait_ge(pv_done, (chunk_no(b, m, c) - 1) * LINES)
                            load_v(m, c)

                    run_slots(sp, slot, CHUNKS, 4, 0)
                    if m == KC:
                        sp.wait_ge(chunk_ready, b * CHUNKS_IMG + 2 * CHUNKS)
                        for u in range(2):
                            sp.dma_start(x_second[:, u], dram_strip(x_tok, b, (0, u))).then_inc(xc_in[u], 16)

                def second_pass(s, inside):
                    if inside(2) and inside(0):
                        sp.wait_ge(mid_done, strip_no(b, s) + 1)
                        u = shifted(s, 2)
                        sp.dma_start(x_second[:, u[1]], dram_strip(x_tok, b, u)).then_inc(xc_in[u[1]], 16)
                    if inside(-2):
                        u = shifted(s, -2)
                        sp.wait_ge(final_done, strip_no(b, u) + 1)
                        sp.dma_start(dram_strip(y_tok, b, u), y_stage[:, u[1]]).then_inc(y_out[u[1]], 16)

                def next_image(slots):
                    for i in slots:
                        one_slot(lambda s, inside: load_first(b + 1, s, inside), i, STRIPS)

                run_slots(sp, second_pass, STRIPS, 2, 2, stop=STRIPS - 1)
                if more:
                    sp.wait_ge(ret_lo, (b + 1) * STRIPS)
                    next_image((-4, -3))
                one_slot(second_pass, STRIPS - 1, STRIPS)
                one_slot(second_pass, STRIPS, STRIPS)
                if more:
                    next_image((-2, -1))
                one_slot(second_pass, STRIPS + 1, STRIPS)

            for i in range(-4, 0):
                one_slot(lambda s, inside: load_first(0, s, inside), i, STRIPS)
            run_images(sp, image, B)
            for u in range(2):
                sp.wait_ge(y_out[u], all_landed(B - 1, u))

        @block.gpsimd
        def _(pool):
            pool.memset(ident[:, :], 0.0).then_inc(ident_clear, 1)
            pool.wait_ge(ident_clear, 1)
            pool.affine_select(out=ident[:, :], in_=ident[:, :], compare_op=ALU.not_equal, fill=1.0,
                               base=0, pattern=[[-1, P]], channel_multiplier=1).then_inc(ident_done, 1)

            def add_row(dst, src, row):
                return pool.tensor_tensor(dst, src, row[:, :].unsqueeze(1).broadcast_to([P, T, C]), ALU.add)

            pool.wait_ge(setup_ready, 1)
            def image(b, more):
                def first_pass(s, inside):
                    pool.wait_ge(v_copied, strip_no(b, s) + 1)
                    add_row(v_stage[:, s[1]], v_stage[:, s[1]], v_bias).then_inc(v_staged, 1)

                run_slots(pool, first_pass, STRIPS, 0, 0)

                def second_pass(s, inside):
                    if inside(1):
                        u = shifted(s, 1)
                        pool.wait_ge(xc_in[u[1]], landed(b, u))
                        add_row(x_second[:, u[1]], x_second[:, u[1]], proj_bias).then_inc(xb_done, 1)
                        pool.wait_ge(ret_hi, strip_no(b, u) + 1)
                        pool.tensor_tensor(ret_t[:, 1], tokens(ret, u), ret_t[:, 0].bitcast(F32),
                                           ALU.subtract).then_inc(ret_lo, 1)
                    if inside(-1):
                        low_act(pool, b, shifted(s, -1), 0)
                    if inside(0):
                        pool.wait_ge(mid_done, strip_no(b, s) + 1)
                        if inside(-2):
                            pool.wait_ge(y_out[s[1]], landed(b, s) - 16)
                        add_row(y_stage[:, s[1]], x_mid[:, s[1]], down_bias).then_inc(base_done, 1)

                run_slots(pool, second_pass, STRIPS, 2, 1)

            run_images(pool, image, B)

        @block.tensor
        def _(pe):
            pe.wait_ge(ident_done, 1)
            pe.wait_ge(dw_in, 32)
            for d in range(2):
                for g in range(KC):
                    for j in range(HG):
                        last = pe.transpose(bank[2 * d + g][:H, j * H:(j + 1) * H],
                                            raw_decay[:, d, g * HG + j, :], ident[:H, :H])
            last.then_inc(setup_pe, 1)
            pe.wait_ge(setup_v, 1)
            for n, w, vec in [(n, raw_qkv, b1) for n in range(2 * KC)] + [(n, raw_up, b2) for n in range(KF)]:
                o = n if w is raw_qkv else 2 * KC + n
                for k in range(KC):
                    pe.matmul(bank[4][:, o:o + 1], w[:, k, n * P:(n + 1) * P], vec[:, k:k + 1],
                              start=(k == 0), stop=(k == KC - 1))
            for k in range(KC):
                last = pe.matmul(bank[5][:, 0:C], ln1_b_cols[:, k, :], raw_qkv[:, k, 2 * C:3 * C],
                                 start=(k == 0), stop=(k == KC - 1))
            last.then_inc(setup_pe, 1)
            pe.wait_ge(setup_ready, 1)

            def transposes(par, x_norm):
                for k in range(KC):
                    for t in range(T):
                        last = pe.transpose(t_bank[par][:, k * STRIP + t * P:k * STRIP + (t + 1) * P],
                                            x_norm[:, par, t, k * P:(k + 1) * P], ident[:, :])
                last.then_inc(t_done, 1)

            def split_product(o, left, right, chunks):
                terms = [(k, a, c) for k in range(chunks) for a, c in ((0, 0), (0, 1), (1, 0))]
                for i, (k, a, c) in enumerate(terms):
                    last = pe.matmul(o, left(a, k), right(c, k), start=(i == 0), stop=(i == len(terms) - 1))
                return last

            def first_pass(b, s, inside):
                if inside(1):
                    u = shifted(s, 1)
                    pe.wait_ge(norm1_done, strip_no(b, u) + 1)
                    transposes(u[1], norm_first)
                if inside(0):
                    pe.wait_ge(lo_done, ln_no(b, 0, s) + 1)
                    if inside(-2):
                        pe.wait_ge(qk_stored, strip_no(b, s) - 1)
                        pe.wait_ge(v_copied, strip_no(b, s) - 1)
                    h = h_t[:, s[1]]
                    for dst, col, signal in ((q_bank, 0, q_done), (k_bank, C, k_done)):
                        for g in range(KC):
                            n = col + g * P
                            last = split_product(dst[s[1]][:, g * STRIP:(g + 1) * STRIP],
                                                 lambda a, k: w_qkv[:, a, k, n:n + P],
                                                 lambda c, k: h[:, c, k, :], KC)
                        last.then_inc(signal, 1)
                    for t in range(T):
                        last = split_product(v_bank[s[1]][:, t * C:(t + 1) * C],
                                             lambda a, k: h[:, a, k, t * P:(t + 1) * P],
                                             lambda c, k: w_qkv[:, c, k, 2 * C:3 * C], KC)
                    last.then_inc(v_done, 1)

            def image(b, more):
                run_slots(pe, lambda s, inside: first_pass(b, s, inside), STRIPS, 2, 1, start=1)

                pe.wait_ge(qk_stored, (b + 1) * STRIPS)
                PAIR = 2 * LINES

                def scores(half, j):
                    c, l = (half + j // PAIR, j % PAIR // LINES), j % LINES
                    if l == 0:
                        pe.wait_ge(chunk_ready, b * CHUNKS_IMG + index(c) + 1)
                    pe.matmul(s_bank[l][:H, 0:HG * H], k_chunk[:, c[1], l * H:(l + 1) * H],
                              q_blocks[:, c[1], :, l * H:(l + 1) * H],
                              start=True, stop=True).then_inc(scores_done, 1)

                def values(half, j, first):
                    c, l = (half, j // LINES), j % LINES
                    n = b * CHUNKS_IMG + index(c)
                    if l == 0:
                        pe.wait_ge(v_in[c[1]], (b * (CHUNKS_IMG // 2) + half + 1) * 16)
                        if not first:
                            pe.wait_ge(o_taken, n - 1)
                    pe.wait_ge(probs_done, n * LINES + l + 1)
                    for e in range(HG):
                        last = pe.matmul(o_bank[c[1]][e * HD:(e + 1) * HD, l * H:(l + 1) * H],
                                         v_chunk[:, c[1], l, e * HD:(e + 1) * HD],
                                         probs[:, l, e * H:(e + 1) * H], start=True, stop=True,
                                         skip_group_check=True)
                    last.then_inc(pv_done, 1)

                LEAD = 2

                def pair(half, first=False, final=False):
                    for j in range(PAIR):
                        if not final or j + LEAD < PAIR:
                            scores(half, j + LEAD)
                        values(half, j, first)

                for j in range(LEAD):
                    scores(0, j)
                pair(0, first=True)
                with pe.Fori(1, CHUNKS_IMG // 2 - 1) as half:
                    pair(half)
                pair(CHUNKS_IMG // 2 - 1, final=True)

                def down(u, bank_used):
                    if bank_used:
                        pe.wait_ge(final_done, strip_no(b, u) - 1)
                    for half in range(2):
                        pe.wait_ge(act_lo[half], strip_no(b, u) + 1)
                        for t in range(T):
                            for k in range(half * KF // 2, (half + 1) * KF // 2):
                                for a, c in ((0, 0), (0, 1), (1, 0)):
                                    last = pe.matmul(down_bank[u[1]][:, t * C:(t + 1) * C],
                                                     act_t[:, a, k, t * P:(t + 1) * P], w_down[:, c, k, :],
                                                     start=(t == 0 and k == 0 and (a, c) == (0, 0)),
                                                     stop=(k == KF - 1 and (a, c) == (1, 0)),
                                                     skip_group_check=True)
                    last.then_inc(down_done, 1)

                def second_pass(s, inside):
                    if inside(0):
                        pe.wait_ge(ret_lo, strip_no(b, s) + 1)
                        for t in range(T):
                            last = split_product(proj_bank[s[1]][:, t * C:(t + 1) * C],
                                                 lambda a, k: ret_t[:, a, k, t * P:(t + 1) * P],
                                                 lambda c, k: w_proj[:, c, k, :], KC)
                        last.then_inc(proj_done, 1)
                    if inside(-1):
                        u = shifted(s, -1)
                        pe.wait_ge(norm2_done, strip_no(b, u) + 1)
                        transposes(u[1], norm_second)
                    if inside(-2):
                        down(shifted(s, -2), inside(-4))
                    if inside(-1):
                        u = shifted(s, -1)
                        pe.wait_ge(lo_done, ln_no(b, 1, u) + 1)
                        for n in range(KF):
                            last = split_product(up_bank[n // 2][:, n % 2 * STRIP:(n % 2 + 1) * STRIP],
                                                 lambda a, k: w_up[:, a, k, n * P:(n + 1) * P],
                                                 lambda c, k: h_t[:, u[1], c, k, :], KC)
                            if n % 2:
                                last.then_inc(up_done, 1)

                run_slots(pe, second_pass, STRIPS, 4, 0, stop=STRIPS + 1)
                if more:
                    one_slot(lambda s, inside: first_pass(b + 1, s, inside), -1, STRIPS)
                    pe.wait_ge(gelu_done, (b + 1) * STRIPS * 2)
                    one_slot(lambda s, inside: first_pass(b + 1, s, inside), 0, STRIPS)
                one_slot(second_pass, STRIPS + 1, STRIPS)
                if more:
                    pe.wait_ge(final_done, (b + 1) * STRIPS)

            for i in range(-1, 1):
                one_slot(lambda s, inside: first_pass(0, s, inside), i, STRIPS)
            run_images(pe, image, B)

        @block.scalar
        def _(act):
            act.wait_ge(setup_ready, 1)

            def high_part(n, par):
                act.wait_ge(t_done, n + 1)
                act.activation(h_t[:, par, 0], t_bank[par][:, :].rearrange("p (k n) -> p k n", k=KC),
                               ACT.Copy).then_inc(hi_done, 1)

            def normalise_first(b, s):
                par = s[1]
                act.wait_ge(shift_done, strip_no(b, s) + 1)
                for t in range(T):
                    last = act.activation(norm_first[:, par, t], x_first[:, par, t], ACT.Identity,
                                          bias=shift[:, par, t:t + 1], scale=rstd[:, par, t:t + 1])
                last.then_inc(norm1_done, 1)

            def image(b, more):
                def prepare(m, c, first=False):
                    g, d = COMBOS[m]
                    if not first:
                        act.wait_ge(scores_done, (chunk_no(b, m, c) - 1) * LINES)
                    act.activation(k_chunk[:, c[1]].rearrange("p (l n) -> p l n", l=LINES),
                                   lines(k_img, g, d, c), ACT.Copy)
                    for e in range(HG):
                        rows = slice(e * HD, (e + 1) * HD)
                        last = act.activation(q_blocks[rows, c[1], e].rearrange("p (l n) -> p l n", l=LINES),
                                              lines(q_img, g, d, c)[rows], ACT.Copy)
                    last.then_inc(chunk_ready, 1)

                def first_pass(s, inside):
                    if inside(1):
                        u = shifted(s, 1)
                        high_part(ln_no(b, 0, u), u[1])
                    if inside(2):
                        normalise_first(b, shifted(s, 2))
                    if inside(0) and not inside(1):
                        act.wait_ge(qk_stored, b * STRIPS + CH // STRIP + 1)
                        prepare(0, (0, 0), first=True)
                    if inside(0):
                        for dst, src, signal, o in ((q_img, q_bank, q_done, 0), (k_img, k_bank, k_done, KC)):
                            act.wait_ge(signal, strip_no(b, s) + 1)
                            for g in range(KC):
                                last = act.activation(dst[:, g, ds(index(s) * STRIP, STRIP)],
                                                      src[s[1]][:, g * STRIP:(g + 1) * STRIP],
                                                      ACT.Identity, bias=qk_bias[:, o + g:o + g + 1])
                        last.then_inc(qk_stored, 1)
                        act.wait_ge(v_done, strip_no(b, s) + 1)
                        if inside(-2):
                            act.wait_ge(v_out[s[1]], landed(b, s) - 16)
                        act.activation(v_stage[:, s[1]], v_bank[s[1]][:, :].rearrange("p (t c) -> p t c", t=T),
                                       ACT.Copy).then_inc(v_copied, 1)

                run_slots(act, first_pass, STRIPS, 2, 2, start=0)

                act.wait_ge(qk_stored, (b + 1) * STRIPS)

                def store_rows(m, c):
                    act.wait_ge(pv_done, (chunk_no(b, m, c) + 1) * LINES)
                    act.activation(ret[:, COMBOS[m][0], ds(index(c) * CH, CH)], o_bank[c[1]][:, 0:CH],
                                   ACT.Copy).then_inc(o_taken, 1)

                for m, (g, d) in enumerate(COMBOS):
                    def slot(c, inside, m=m, d=d):
                        if inside(0) and inside(1):
                            prepare(m, shifted(c, 1), first=(m == 0 and not inside(-1)))
                        elif inside(0) and m + 1 < len(COMBOS):
                            prepare(m + 1, (0, 0))
                        if inside(-1) and d == ROWS:
                            store_rows(m, shifted(c, -1))

                    run_slots(act, slot, CHUNKS, 1, 1)

                act.wait_ge(o_taken, (b + 1) * CHUNKS_IMG)

                def second_pass(s, inside):
                    if inside(-1):
                        u = shifted(s, -1)
                        high_part(ln_no(b, 1, u), u[1])
                    if inside(1):
                        u = shifted(s, 1)
                        if inside(0):
                            act.wait_ge(proj_done, strip_no(b, u))
                        act.activation(ret_t[:, 0], tokens(ret, u), ACT.Copy).then_inc(ret_hi, 1)
                    if more and inside(-1) and not inside(0):
                        for u in range(2):
                            normalise_first(b + 1, (0, u))
                    if inside(-1):
                        n = strip_no(b, shifted(s, -1))
                        for half in range(2):
                            ks = range(half * KF // 2, (half + 1) * KF // 2)
                            act.wait_ge(up_done, 2 * n + half + 1)
                            for i, k in enumerate(ks):
                                last = act.activation(act_f[:, k], up_bank[half][:, i * STRIP:(i + 1) * STRIP],
                                                      ACT.Gelu, bias=up_bias[:, k:k + 1])
                            last.then_inc(gelu_done, 1)
                            act.wait_ge(gelu_done, 2 * n + half + 1)
                            act.activation(act_t[:, 0, ks[0]:ks[-1] + 1], act_f[:, ks[0]:ks[-1] + 1],
                                           ACT.Copy).then_inc(act_hi, 1)

                run_slots(act, second_pass, STRIPS, 1, 1)
                if more:
                    high_part(ln_no(b + 1, 0, (0, 0)), 0)

            for u in range(2):
                normalise_first(0, (0, u))
            high_part(0, 0)
            run_images(act, image, B)

        @block.vector
        def _(dve):
            links = [0]

            def link(ins):
                links[0] += 1
                ins.then_inc(setup_link, 1)
                dve.wait_ge(setup_link, links[0])

            dve.memset(q_blocks[:, :, :, :], 0.0)
            dve.wait_ge(ident_done, 1)
            dve.wait_ge(w_in, 14 * 16)
            for k in range(KC):
                last = dve.tensor_scalar(ln1_b_cols[:, k, :], ident[:, :], 0.0, b1[:, k:k + 1], ALU.mult, ALU.add)
            last.then_inc(setup_v, 1)
            for raw, w, gain in ((raw_qkv, w_qkv, g1), (raw_up, w_up, g2)):
                for k in range(KC):
                    link(dve.tensor_scalar(w[:, 0, k], raw[:, k], gain[:, k:k + 1], None, ALU.mult))
                    dve.scalar_tensor_tensor(out=w[:, 1, k], in0=raw[:, k], scalar=gain[:, k:k + 1],
                                             in1=w[:, 0, k].bitcast(F32), op0=ALU.mult, op1=ALU.subtract)
            link(dve.tensor_tensor(proj_scaled, raw_proj, gamma_row.unsqueeze(1).broadcast_to([P, KC, C]), ALU.mult))
            for raw, w in ((proj_scaled, w_proj), (raw_down, w_down)):
                link(dve.tensor_copy(w[:, 0], raw))
                dve.tensor_tensor(w[:, 1], raw, w[:, 0].bitcast(F32), ALU.subtract)
            dve.tensor_tensor(proj_bias[:, :], proj_bias[:, :], gamma_row, ALU.mult)
            dve.wait_ge(setup_pe, 1)
            for d in range(2):
                for g in range(KC):
                    dve.tensor_scalar(decay[:, d, g], bank[2 * d + g][:H, 0:HG * H], 0.5, None, ALU.mult)
            dve.wait_ge(setup_pe, 2)
            dve.tensor_tensor(qk_bias[:, :], bank[4][:, 0:2 * KC], raw_qk_bias, ALU.add)
            dve.tensor_tensor(up_bias[:, :], bank[4][:, 2 * KC:2 * KC + KF], raw_up_bias, ALU.add)
            dve.tensor_tensor(v_bias[:, :], bank[5][:, 0:C], v_bias[:, :], ALU.add).then_inc(setup_ready, 1)
            dve.wait_ge(setup_ready, 1)

            def statistics(n, par, src):
                for t in range(T):
                    dve.bn_stats(bn[:, par, t], src[:, t]).then_inc(bn_done, 1)
                dve.wait_ge(bn_done, (n + 1) * T)
                dve.sem_inc(bn_seen, 1)
                for t in range(T):
                    dve.bn_aggr(mean_var[:, par, t], bn[:, par, t]).then_inc(mv_done, 1)
                dve.wait_ge(mv_done, (n + 1) * T)
                dve.tensor_scalar(var_eps[:, par], mean_var[:, par, :, 1], EPS, None, ALU.add).then_inc(ve_done, 1)
                dve.tensor_scalar(neg_half[:, par], mean_var[:, par, :, 1], EPS, -0.5, ALU.add,
                                  ALU.mult).then_inc(ve_done, 1)
                dve.wait_ge(ve_done, 2 * n + 2)
                y, t = rstd[:, par], newton[:, par]
                dve.tensor_scalar(y.bitcast(I32), var_eps[:, par].bitcast(I32), -0.5, RSQRT_SEED,
                                  ALU.mult, ALU.add).then_inc(newton_step, 1)
                done = 1
                for _ in range(NEWTON_STEPS):
                    for step in (lambda: dve.tensor_tensor(t, y, y, ALU.mult),
                                 lambda: dve.tensor_tensor(t, t, neg_half[:, par], ALU.mult),
                                 lambda: dve.scalar_tensor_tensor(out=y, in0=t, scalar=1.5, in1=y,
                                                                  op0=ALU.add, op1=ALU.mult)):
                        dve.wait_ge(newton_step, n * (3 * NEWTON_STEPS + 1) + done)
                        step().then_inc(newton_step, 1)
                        done += 1

            def statistics_first(b, s):
                n, par = ln_no(b, 0, s), s[1]
                dve.wait_ge(xa_in[par], landed(b, s))
                statistics(n, par, x_first[:, par])
                dve.wait_ge(newton_step, (n + 1) * (3 * NEWTON_STEPS + 1))
                dve.scalar_tensor_tensor(out=shift[:, par], in0=mean_var[:, par, :, 0], scalar=-1.0,
                                         in1=rstd[:, par], op0=ALU.mult, op1=ALU.mult).then_inc(shift_done, 1)

            def normalise(n, par, src, x_norm):
                dve.wait_ge(newton_step, (n + 1) * (3 * NEWTON_STEPS + 1))
                for t in range(T):
                    last = dve.tensor_scalar(x_norm[:, par, t], src[:, t], mean_var[:, par, t, 0:1],
                                             rstd[:, par, t:t + 1], ALU.subtract, ALU.mult)
                last.then_inc(norm2_done, 1)

            def low_part(n, par):
                dve.wait_ge(hi_done, n + 1)
                dve.tensor_tensor(h_t[:, par, 1], t_bank[par][:, :].rearrange("p (k n) -> p k n", k=KC),
                                  h_t[:, par, 0].bitcast(F32), ALU.subtract).then_inc(lo_done, 1)

            def first_pass(b, s, inside):
                if inside(1):
                    u = shifted(s, 1)
                    low_part(ln_no(b, 0, u), u[1])
                if inside(3):
                    statistics_first(b, shifted(s, 3))

            def image(b, more):
                run_slots(dve, lambda s, inside: first_pass(b, s, inside), STRIPS, 0, 3, start=1)

                def add_columns(m, c):
                    g = COMBOS[m][0]
                    dve.wait_ge(pv_done, (chunk_no(b, m, c) + 1) * LINES)
                    dve.tensor_tensor(lines(ret, g, COLS, c),
                                      o_bank[c[1]][:, 0:CH].rearrange("p (l n) -> p l n", l=LINES),
                                      lines(ret, g, COLS, c), ALU.add).then_inc(o_taken, 1)

                LAST = ((CHUNKS - 1) // 2, (CHUNKS - 1) % 2)
                for m, (g, d) in enumerate(COMBOS):
                    def slot(c, inside, m=m, g=g, d=d):
                        if not inside(0):
                            return
                        n = chunk_no(b, m, c)
                        for l in range(LINES):
                            if l == LINES // 2:
                                if inside(-1) and d == COLS:
                                    if not inside(-2):
                                        dve.wait_ge(o_taken, b * CHUNKS_IMG + m * CHUNKS)
                                    add_columns(m, shifted(c, -1))
                                elif not inside(-1) and m and d == ROWS:
                                    add_columns(m - 1, LAST)
                            dve.wait_ge(scores_done, n * LINES + l + 1)
                            if m or inside(-1):
                                dve.wait_ge(pv_done, n * LINES + l + 1 - LINES)
                            dve.tensor_tensor(probs[:, l], s_bank[l][:H, 0:HG * H], decay[:, d, g],
                                              ALU.mult).then_inc(probs_done, 1)

                    run_slots(dve, slot, CHUNKS, 2, 0)
                add_columns(len(COMBOS) - 1, LAST)

                def final_sum(u):
                    dve.wait_ge(down_done, strip_no(b, u) + 1)
                    dve.wait_ge(base_done, strip_no(b, u) + 1)
                    dve.tensor_tensor(y_stage[:, u[1]], down_bank[u[1]][:, :].rearrange("p (t c) -> p t c", t=T),
                                      y_stage[:, u[1]], ALU.add).then_inc(final_done, 1)

                def second_pass(s, inside):
                    if inside(-2):
                        low_act(dve, b, shifted(s, -2), 1)
                    if inside(0):
                        n = strip_no(b, s)
                        dve.wait_ge(proj_done, n + 1)
                        dve.wait_ge(xb_done, n + 1)
                        if inside(-2):
                            dve.wait_ge(base_done, n - 1)
                        dve.tensor_tensor(x_mid[:, s[1]], proj_bank[s[1]][:, :].rearrange("p (t c) -> p t c", t=T),
                                          x_second[:, s[1]], ALU.add).then_inc(mid_done, 1)
                    if inside(-1):
                        u = shifted(s, -1)
                        low_part(ln_no(b, 1, u), u[1])
                    if inside(0):
                        dve.wait_ge(mid_done, strip_no(b, s) + 1)
                        statistics(ln_no(b, 1, s), s[1], x_mid[:, s[1]])
                        normalise(ln_no(b, 1, s), s[1], x_mid[:, s[1]], norm_second)
                    if inside(-2):
                        final_sum(shifted(s, -2))

                run_slots(dve, second_pass, STRIPS, 2, 0, stop=STRIPS)
                if more:
                    for u in range(2):
                        statistics_first(b + 1, (0, u))
                one_slot(second_pass, STRIPS, STRIPS)
                if more:
                    one_slot(lambda s, inside: first_pass(b + 1, s, inside), -1, STRIPS)
                tail = ((STRIPS - 1) // 2, (STRIPS - 1) % 2)
                low_act(dve, b, tail, 1)
                if more:
                    one_slot(lambda s, inside: first_pass(b + 1, s, inside), 0, STRIPS)
                final_sum(tail)

            for u in range(2):
                statistics_first(0, (0, u))
            for i in range(-1, 1):
                one_slot(lambda s, inside: first_pass(0, s, inside), i, STRIPS)
            run_images(dve, image, B)


NAMES = ("x", "L0_conv_decay_h", "L0_conv_decay_w", "L0_conv_qkv_w", "L0_conv_qkv_b", "L0_conv_proj_w",
         "L0_conv_proj_b", "L0_conv_ln1_g", "L0_conv_ln1_b", "L0_conv_ln2_g", "L0_conv_ln2_b",
         "L0_conv_ffn_w1", "L0_conv_ffn_b1", "L0_conv_ffn_w2", "L0_conv_ffn_b2", "L0_conv_gamma")


def kernel(**inputs):
    import numpy as np
    import concourse.bacc as bacc
    from concourse.bass_utils import run_bass_kernel_spmd

    nc = bacc.Bacc("TRN2", target_bir_lowering=False, num_devices=1)
    arrays, args = {}, []
    for name in NAMES:
        a = np.ascontiguousarray(inputs[name])
        arrays[f"in_{name}"] = a
        args.append(nc.dram_tensor(f"in_{name}", a.shape, F32, kind="ExternalInput").ap())
    shape = inputs["x"].shape
    v_rows = nc.dram_tensor("v_rows", shape, F32, kind="Internal").ap()
    out = nc.dram_tensor("out", shape, F32, kind="ExternalOutput").ap()
    build(nc, *args, v_rows, out)
    result = run_bass_kernel_spmd(nc, [arrays], core_ids=[0])
    return result.results[0]["out"]
```

```python
from contextlib import ExitStack

import concourse.bass as bass
from concourse import mybir

ALU = mybir.AluOpType
ACT = mybir.ActivationFunctionType
F32 = mybir.dt.float32
F32R = mybir.dt.float32r
I32 = mybir.dt.int32
ds = bass.ds

P = 128
HEADS = 8
EPS = 1e-5
RSQRT_SEED = float(0x5F3759DF)
NEWTON_STEPS = 3


def shifted(unit, k):
    half, par = unit
    return half + (par + k) // 2, (par + k) % 2


def index(unit):
    return 2 * unit[0] + unit[1]


def one_slot(slot, s, count):
    slot((s // 2, s % 2), lambda k: 0 <= s + k < count)


def run_slots(eng, slot, count, back, ahead, start=None, stop=None):
    start = -ahead if start is None else start
    stop = count + back if stop is None else stop
    first = max(back + back % 2, start + start % 2)
    last = (count - ahead) // 2 * 2
    for s in range(start, first):
        one_slot(slot, s, count)
    with eng.Fori(first // 2, last // 2) as half:
        for par in range(2):
            slot((half, par), lambda k: True)
    for s in range(last, stop):
        one_slot(slot, s, count)


def run_images(eng, image, images):
    with eng.Fori(0, images - 1) as b:
        image(b, True)
    image(images - 1, False)


def build(nc, x, decay_h, decay_w, qkv_w, qkv_b, proj_w, proj_b, ln1_g, ln1_b, ln2_g, ln2_b,
          ffn_w1, ffn_b1, ffn_w2, ffn_b2, gamma, v_rows, out):
    B, H, W, C = x.shape
    assert H == W and C == 2 * P and H % 8 == 0
    N = H * W
    KC = C // P
    HD = C // HEADS
    HG = HEADS // KC
    FF = ffn_w1.shape[1]
    KF = FF // P
    T = 2
    STRIP = T * P
    STRIPS = N // STRIP
    LINES = 4
    CH = LINES * W
    CHUNKS = H // LINES
    ROWS, COLS = 1, 0
    COMBOS = [(0, ROWS), (0, COLS), (1, COLS), (1, ROWS)]
    assert KC == 2
    CHUNKS_IMG = len(COMBOS) * CHUNKS
    LAST = ((CHUNKS - 1) // 2, (CHUNKS - 1) % 2)
    PAIR = 2
    PAIRS = LINES // PAIR
    HI_ACT, HI_DVE = (0, 1), (2, 3)
    LO_SP = (0,)
    LO_ACT, LO_DVE = ((1,), (1, 2)), ((2, 3), (3,))
    assert N % STRIP == 0 and CHUNKS % 2 == 0 and HD == 32

    with ExitStack() as ctx:
        def sb(name, shape, dt=F32):
            return ctx.enter_context(nc.sbuf_tensor(name, shape, dt))

        def sem(name):
            return ctx.enter_context(nc.semaphore(name))

        img = sb("img", [P, 3 * KC - 1, N])
        img_end = nc.sbuf_base
        ret, q_img, k_img = img[:, 0:KC], img[:, KC - 1:2 * KC - 1], img[:, 2 * KC - 1:3 * KC - 1]

        def strip_buffers(region, n):
            w = 2 * T * C
            return [region[:, i * w:(i + 1) * w].rearrange("p (u t c) -> p u t c", u=2, t=T) for i in range(n)]

        x_first, norm_first, v_stage = strip_buffers(img[:, 0], 3)
        x_second, norm_second, x_mid, y_stage = strip_buffers(k_img[:, 0], 4)
        act_f = k_img[:, 0, 8 * T * C:8 * T * C + KF * STRIP].rearrange("p (k n) -> p k n", k=KF)
        w_qkv = sb("w_qkv", [P, 2, KC, 3 * C], F32R)
        w_proj = sb("w_proj", [P, 2, KC, C], F32R)
        w_up = sb("w_up", [P, 2, KC, FF], F32R)
        w_down = sb("w_down", [P, 2, KF, C], F32R)
        h_t = sb("h_t", [P, 2, 2, KC, STRIP], F32R)
        q1_end = img_end - KC * N * 4
        ret_t = nc.alloc_sbuf_tensor_at("ret_t", [P, 2, KC, STRIP], F32R, offset=q1_end - N * 4)
        act_t = nc.alloc_sbuf_tensor_at("act_t", [P, 2, KF, STRIP], F32R, offset=q1_end - 2 * KF * STRIP * 4)
        decay = sb("decay", [H, 2, KC, HG * H])
        ident = sb("ident", [P, P])
        v_bias = sb("v_bias", [P, C])
        proj_bias = sb("proj_bias", [P, C])
        down_bias = sb("down_bias", [P, C])
        qk_bias = sb("qk_bias", [P, 2 * KC])
        up_bias = sb("up_bias", [P, KF])
        q_blocks = sb("q_blocks", [P, 2, 2, HG, CH], F32R)
        k_chunk = sb("k_chunk", [P, 2, 2, CH], F32R)
        v_chunk = sb("v_chunk", [H, 2, LINES, P])
        probs = sb("probs", [H, LINES, HG * H])
        bn = sb("bn", [P, 2, T, 6])
        mean_var = sb("mean_var", [P, 2, T, 2])
        var_eps = sb("var_eps", [P, 2, T])
        neg_half = sb("neg_half", [P, 2, T])
        rstd = sb("rstd", [P, 2, T])
        newton = sb("newton", [P, 2, T])
        shift = sb("shift", [P, 2, T])

        scores_all = ctx.enter_context(nc.psum_tensor("scores_all", [P, LINES, 512], F32))
        bank = [scores_all[:, i] for i in range(LINES)]
        bank += [ctx.enter_context(nc.psum_tensor(f"bank{i}", [P, 512], F32)) for i in range(LINES, 8)]
        t_bank = bank[0:2]
        q_bank, k_bank, v_bank = (bank[2], bank[4]), (bank[3], bank[5]), bank[6:8]
        proj_bank, up_bank, down_bank = bank[6:8], bank[2:4], bank[4:6]
        o_bank = bank[4:6]

        w_in, dw_in = sem("w_in"), sem("dw_in")
        ident_clear, ident_done = sem("ident_clear"), sem("ident_done")
        setup_v, setup_pe, setup_ready = sem("setup_v"), sem("setup_pe"), sem("setup_ready")
        blocks_clear = sem("blocks_clear")
        setup_link = sem("setup_link")
        sp_steps, bn_seen = sem("sp_steps"), sem("bn_seen")
        xa_in = [sem(f"xa_in{u}") for u in range(2)]
        xc_in = [sem(f"xc_in{u}") for u in range(2)]
        bn_done, mv_done, ve_done = sem("bn_done"), sem("mv_done"), sem("ve_done")
        newton_step, shift_done = sem("newton_step"), sem("shift_done")
        norm1_done, norm2_done = sem("norm1_done"), sem("norm2_done")
        t_done, hi_done, lo_done = sem("t_done"), sem("hi_done"), sem("lo_done")
        q_done, k_done, v_done = sem("q_done"), sem("k_done"), sem("v_done")
        qk_stored, v_copied, v_staged = sem("qk_stored"), sem("v_copied"), sem("v_staged")
        v_out = [sem(f"v_out{u}") for u in range(2)]
        v_in = [sem(f"v_in{u}") for u in range(2)]
        q_rounded, q_rest, k_rounded, k_rest = sem("q_rounded"), sem("q_rest"), sem("k_rounded"), sem("k_rest")
        heads_act, heads_dve = sem("heads_act"), sem("heads_dve")
        rest_in = [sem(f"rest_in{u}") for u in range(2)]
        scores_done, probs_done = sem("scores_done"), sem("probs_done")
        pv_done, o_taken = sem("pv_done"), sem("o_taken")
        xb_done, ret_hi, ret_lo, proj_done = sem("xb_done"), sem("ret_hi"), sem("ret_lo"), sem("proj_done")
        mid_done, base_done = sem("mid_done"), sem("base_done")
        up_done, gelu_done, act_hi = sem("up_done"), sem("gelu_done"), sem("act_hi")
        act_lo = [sem(f"act_lo{u}") for u in range(2)]
        down_done, final_done = sem("down_done"), sem("final_done")
        y_out = [sem(f"y_out{u}") for u in range(2)]

        def strip_no(b, s):
            return b * STRIPS + index(s)

        def ln_no(b, phase, s):
            return b * 2 * STRIPS + phase * STRIPS + index(s)

        def chunk_no(b, m, c):
            return b * CHUNKS_IMG + m * CHUNKS + index(c)

        def landed(b, s):
            return (b * ((STRIPS + 1 - s[1]) // 2) + s[0] + 1) * 16

        def all_landed(b, par):
            return (b + 1) * ((STRIPS + 1 - par) // 2) * 16

        x_tok = x.rearrange("b h w c -> (b h w) c").rearrange("(s t p) c -> s p t c", t=T, p=P)
        y_tok = out.rearrange("b h w c -> (b h w) c").rearrange("(s t p) c -> s p t c", t=T, p=P)
        v_tok = v_rows.rearrange("b h w c -> (b h w) c").rearrange("(s t p) c -> s p t c", t=T, p=P)

        def dram_strip(view, b, s):
            return view[ds(strip_no(b, s), 1)].rearrange("s p t c -> p (s t) c")

        def tokens(img, s):
            return img[:, :, ds(index(s) * STRIP, STRIP)]

        def lines(img, g, d, c):
            if d:
                return img[:, g, ds(index(c) * CH, CH)].rearrange("p (l n) -> p l n", l=LINES)
            return img[:, g].rearrange("p (h w) -> p w h", w=W)[:, ds(index(c) * LINES, LINES)]

        raw_q = q_img.rearrange("p k n -> p (k n)")
        at = [0]

        def staging(rows, n):
            at[0] += n
            return raw_q[:rows, at[0] - n:at[0]]

        raw_qkv = staging(P, KC * 3 * C).rearrange("p (k n) -> p k n", k=KC)
        raw_proj = staging(P, KC * C).rearrange("p (k n) -> p k n", k=KC)
        raw_up = staging(P, KC * FF).rearrange("p (k n) -> p k n", k=KC)
        raw_down = staging(P, KF * C).rearrange("p (k n) -> p k n", k=KF)
        raw_decay = staging(H, 2 * HEADS * H).rearrange("p (d e n) -> p d e n", d=2, e=HEADS)
        proj_scaled = staging(P, KC * C).rearrange("p (k n) -> p k n", k=KC)
        gamma_row = staging(P, C)
        ln1_b_cols = staging(P, KC * P).rearrange("p (k n) -> p k n", k=KC)
        g1, b1, g2, b2 = (staging(P, KC) for _ in range(4))
        raw_qk_bias, raw_up_bias = staging(P, 2 * KC), staging(P, KF)

        def low_act(eng, b, s, half):
            ks = slice(half * KF // 2, (half + 1) * KF // 2)
            eng.wait_ge(act_hi, 2 * strip_no(b, s) + half + 1)
            eng.tensor_tensor(act_t[:, 1, ks], act_f[:, ks], act_t[:, 0, ks].bitcast(F32),
                              ALU.subtract).then_inc(act_lo[half], 1)

        def q_part(c, a):
            return h_t[:, (c[1] + STRIPS) % 2, a].rearrange("p k n -> p (k n)")[:, :CH]

        def following(m, c, inside, k):
            if inside(k):
                return m, shifted(c, k)
            first = index(c) + k - CHUNKS
            return (m + 1, (first // 2, first % 2)) if m + 1 < len(COMBOS) else None

        def by_line(v):
            return v.rearrange("p (l n) -> p l n", l=LINES)

        def copy_heads(copy, c, a, heads):
            for e in heads:
                rows = slice(e * HD, (e + 1) * HD)
                last = copy(q_blocks[rows, c[1], a, e], q_part(c, a)[rows])
            return last

        block = ctx.enter_context(nc.Block())

        @block.sync
        def _(sp):
            def by_chunk(v, k):
                return v.rearrange("(k p) -> p k", k=k)

            def hold():
                sp.sem_inc(sp_steps, 1)

            def load_first(b, s, inside):
                if inside(2):
                    sp.wait_ge(norm1_done, strip_no(b, shifted(s, 2)) + 1)
                u = shifted(s, 4)
                sp.dma_start(x_first[:, u[1]], dram_strip(x_tok, b, u)).then_inc(xa_in[u[1]], 16)

            for i in range(-4, -2):
                one_slot(lambda s, inside: load_first(0, s, inside), i, STRIPS)
            for dst, src in ((raw_qkv, qkv_w.rearrange("(k p) n -> p k n", p=P)),
                             (raw_proj, proj_w.rearrange("(k p) n -> p k n", p=P)),
                             (raw_up, ffn_w1.rearrange("(k p) n -> p k n", p=P)),
                             (raw_down, ffn_w2.rearrange("(k p) n -> p k n", p=P)),
                             (g1, by_chunk(ln1_g, KC)), (b1, by_chunk(ln1_b, KC)),
                             (g2, by_chunk(ln2_g, KC)), (b2, by_chunk(ln2_b, KC)),
                             (raw_qk_bias, by_chunk(qkv_b[0:2 * C], 2 * KC)),
                             (raw_up_bias, by_chunk(ffn_b1, KF)),
                             (v_bias[:, :], qkv_b[2 * C:3 * C].partition_broadcast(P)),
                             (proj_bias[:, :], proj_b.partition_broadcast(P)),
                             (down_bias[:, :], ffn_b2.partition_broadcast(P)),
                             (gamma_row, gamma.partition_broadcast(P))):
                sp.dma_start(dst, src, allow_slow_non_contiguous=True).then_inc(w_in, 16)
            for d, src in enumerate((decay_h, decay_w)):
                sp.dma_start(raw_decay[:, d], src.rearrange("e q k -> q e k")).then_inc(dw_in, 16)

            def image(b, more):
                def load_v(m, c):
                    g, d = COMBOS[m]
                    v_img = v_rows[ds(b, 1), :, :, g * P:(g + 1) * P].rearrange("b h w c -> (b h) w c")
                    span = ds(index(c) * LINES, LINES)
                    src = v_img[span].rearrange("l p c -> p l c") if d == ROWS else v_img[:, span]
                    sp.dma_start(v_chunk[:, c[1]], src).then_inc(v_in[c[1]], 16)

                def rest_of_q(m, c, first):
                    n = chunk_no(b, m, c)
                    sp.wait_ge(q_rest, n + 1)
                    if not first:
                        hold()
                        sp.wait_ge(scores_done, (n - 1) * PAIRS)
                    for e in LO_SP:
                        rows = slice(e * HD, (e + 1) * HD)
                        sp.dma_start(q_blocks[rows, c[1], 1, e].bitcast(F32),
                                     q_part(c, 1)[rows].bitcast(F32)).then_inc(rest_in[c[1]], 16)

                def stage_v(s, inside):
                    if inside(4):
                        load_first(b, s, inside)
                    if inside(1) and not inside(2):
                        sp.wait_ge(v_out[0], landed(b, (1, 0)))
                        sp.wait_ge(v_out[1], landed(b, (0, 1)))
                        for c in range(2):
                            load_v(0, (0, c))
                    if inside(0) and not inside(1):
                        for c in range(2):
                            rest_of_q(0, (0, c), first=True)
                    if inside(0):
                        sp.wait_ge(v_staged, strip_no(b, s) + 1)
                        sp.dma_start(dram_strip(v_tok, b, s), v_stage[:, s[1]]).then_inc(v_out[s[1]], 16)

                run_slots(sp, stage_v, STRIPS, 0, 4, start=0)

                for m in range(len(COMBOS)):
                    def slot(c, inside, m=m):
                        if inside(0) and (m or inside(-2)):
                            rest_of_q(m, c, first=False)
                        if m == 0 and inside(-2) and not inside(-3):
                            for u in range(2):
                                sp.wait_ge(v_out[u], all_landed(b, u))
                            hold()
                        if inside(0) and (m or inside(-2)):
                            sp.wait_ge(pv_done, (chunk_no(b, m, c) - 1) * PAIRS)
                            load_v(m, c)

                    run_slots(sp, slot, CHUNKS, 4, 0)
                    if m == KC:
                        sp.wait_ge(k_rest, b * CHUNKS_IMG + 2 * CHUNKS)
                        for u in range(2):
                            sp.dma_start(x_second[:, u], dram_strip(x_tok, b, (0, u))).then_inc(xc_in[u], 16)

                def second_pass(s, inside):
                    if inside(2) and inside(0):
                        sp.wait_ge(mid_done, strip_no(b, s) + 1)
                        u = shifted(s, 2)
                        sp.dma_start(x_second[:, u[1]], dram_strip(x_tok, b, u)).then_inc(xc_in[u[1]], 16)
                    if inside(-2):
                        u = shifted(s, -2)
                        sp.wait_ge(final_done, strip_no(b, u) + 1)
                        sp.dma_start(dram_strip(y_tok, b, u), y_stage[:, u[1]]).then_inc(y_out[u[1]], 16)

                def next_image(slots):
                    for i in slots:
                        one_slot(lambda s, inside: load_first(b + 1, s, inside), i, STRIPS)

                run_slots(sp, second_pass, STRIPS, 2, 2, stop=STRIPS - 2)
                if more:
                    sp.wait_ge(ret_lo, b * STRIPS + 3 * 2 * T * C // STRIP)
                    next_image((-4, -3))
                one_slot(second_pass, STRIPS - 2, STRIPS)
                one_slot(second_pass, STRIPS - 1, STRIPS)
                one_slot(second_pass, STRIPS, STRIPS)
                if more:
                    next_image((-2, -1))
                one_slot(second_pass, STRIPS + 1, STRIPS)

            for i in range(-2, 0):
                one_slot(lambda s, inside: load_first(0, s, inside), i, STRIPS)
            run_images(sp, image, B)
            for u in range(2):
                sp.wait_ge(y_out[u], all_landed(B - 1, u))

        @block.gpsimd
        def _(pool):
            pool.memset(ident[:, :], 0.0).then_inc(ident_clear, 1)
            pool.memset(q_blocks[:, :, :, :, :].bitcast(F32), 0.0).then_inc(blocks_clear, 1)
            pool.wait_ge(ident_clear, 1)
            pool.affine_select(out=ident[:, :], in_=ident[:, :], compare_op=ALU.not_equal, fill=1.0,
                               base=0, pattern=[[-1, P]], channel_multiplier=1).then_inc(ident_done, 1)

            def add_row(dst, src, row):
                return pool.tensor_tensor(dst, src, row[:, :].unsqueeze(1).broadcast_to([P, T, C]), ALU.add)

            pool.wait_ge(setup_ready, 1)

            def image(b, more):
                def low_q(m, c):
                    g, d = COMBOS[m]
                    n = chunk_no(b, m, c)
                    pool.wait_ge(q_rounded, n + 1)
                    pool.tensor_tensor(by_line(q_part(c, 1)), lines(q_img, g, d, c),
                                       by_line(q_part(c, 0).bitcast(F32)), ALU.subtract).then_inc(q_rest, 1)

                def low_k(m, c):
                    g, d = COMBOS[m]
                    n = chunk_no(b, m, c)
                    pool.wait_ge(k_rounded, n + 1)
                    pool.tensor_tensor(by_line(k_chunk[:, c[1], 1]), lines(k_img, g, d, c),
                                       by_line(k_chunk[:, c[1], 0].bitcast(F32)), ALU.subtract).then_inc(k_rest, 1)

                def first_pass(s, inside):
                    if not inside(1):
                        low_q(0, (0, 0))
                        low_k(0, (0, 0))
                        low_q(0, (0, 1))
                    pool.wait_ge(v_copied, strip_no(b, s) + 1)
                    add_row(v_stage[:, s[1]], v_stage[:, s[1]], v_bias).then_inc(v_staged, 1)

                run_slots(pool, first_pass, STRIPS, 0, 1, start=0)
                low_k(0, (0, 1))
                for m in range(len(COMBOS)):
                    def low_parts(c, inside, m=m):
                        low_q(m, c)
                        low_k(m, c)

                    run_slots(pool, low_parts, CHUNKS, 0, 0, start=0 if m else 2)

                def second_pass(s, inside):
                    if inside(1):
                        u = shifted(s, 1)
                        pool.wait_ge(xc_in[u[1]], landed(b, u))
                        add_row(x_second[:, u[1]], x_second[:, u[1]], proj_bias).then_inc(xb_done, 1)
                        pool.wait_ge(ret_hi, strip_no(b, u) + 1)
                        pool.tensor_tensor(ret_t[:, 1], tokens(ret, u), ret_t[:, 0].bitcast(F32),
                                           ALU.subtract).then_inc(ret_lo, 1)
                    if inside(-1):
                        u = shifted(s, -1)
                        pool.wait_ge(mid_done, strip_no(b, u) + 1)
                        if inside(-3):
                            pool.wait_ge(y_out[u[1]], landed(b, u) - 16)
                        add_row(y_stage[:, u[1]], x_mid[:, u[1]], down_bias).then_inc(base_done, 1)
                        low_act(pool, b, u, 0)

                run_slots(pool, second_pass, STRIPS, 3, 1, stop=STRIPS + 1)

            run_images(pool, image, B)

        @block.tensor
        def _(pe):
            pe.wait_ge(ident_done, 1)
            pe.wait_ge(setup_v, 1)
            for n, w, vec in [(n, raw_qkv, b1) for n in range(2 * KC)] + [(n, raw_up, b2) for n in range(KF)]:
                o = n if w is raw_qkv else 2 * KC + n
                for k in range(KC):
                    pe.matmul(bank[4][:, o:o + 1], w[:, k, n * P:(n + 1) * P], vec[:, k:k + 1],
                              start=(k == 0), stop=(k == KC - 1))
            for k in range(KC):
                last = pe.matmul(bank[5][:, 0:C], ln1_b_cols[:, k, :], raw_qkv[:, k, 2 * C:3 * C],
                                 start=(k == 0), stop=(k == KC - 1))
            last.then_inc(setup_pe, 1)
            pe.wait_ge(dw_in, 32)
            for d in range(2):
                for g in range(KC):
                    for j in range(HG):
                        last = pe.transpose(bank[2 * d + g][:H, j * H:(j + 1) * H],
                                            raw_decay[:, d, g * HG + j, :], ident[:H, :H])
            last.then_inc(setup_pe, 1)
            pe.wait_ge(setup_ready, 1)

            def transposes(par, x_norm):
                for k in range(KC):
                    for t in range(T):
                        last = pe.transpose(t_bank[par][:, k * STRIP + t * P:k * STRIP + (t + 1) * P],
                                            x_norm[:, par, t, k * P:(k + 1) * P], ident[:, :])
                last.then_inc(t_done, 1)

            def split_product(o, left, right, chunks):
                terms = [(k, a, c) for k in range(chunks) for a, c in ((0, 0), (0, 1), (1, 0))]
                for i, (k, a, c) in enumerate(terms):
                    last = pe.matmul(o, left(a, k), right(c, k), start=(i == 0), stop=(i == len(terms) - 1))
                return last

            def first_pass(b, s, inside):
                if inside(1):
                    u = shifted(s, 1)
                    pe.wait_ge(norm1_done, strip_no(b, u) + 1)
                    transposes(u[1], norm_first)
                if inside(0):
                    pe.wait_ge(lo_done, ln_no(b, 0, s) + 1)
                    if inside(-2):
                        pe.wait_ge(qk_stored, strip_no(b, s) - 1)
                        pe.wait_ge(v_copied, strip_no(b, s) - 1)
                    h = h_t[:, s[1]]
                    for dst, col, signal in ((q_bank, 0, q_done), (k_bank, C, k_done)):
                        for g in range(KC):
                            n = col + g * P
                            last = split_product(dst[s[1]][:, g * STRIP:(g + 1) * STRIP],
                                                 lambda a, k: w_qkv[:, a, k, n:n + P],
                                                 lambda c, k: h[:, c, k, :], KC)
                        last.then_inc(signal, 1)
                    for t in range(T):
                        last = split_product(v_bank[s[1]][:, t * C:(t + 1) * C],
                                             lambda a, k: h[:, a, k, t * P:(t + 1) * P],
                                             lambda c, k: w_qkv[:, c, k, 2 * C:3 * C], KC)
                    last.then_inc(v_done, 1)

            def image(b, more):
                run_slots(pe, lambda s, inside: first_pass(b, s, inside), STRIPS, 2, 1, start=1)

                def scores(half, j):
                    c, p = (half + j // (2 * PAIRS), j % (2 * PAIRS) // PAIRS), j % PAIRS
                    if p == 0:
                        n = b * CHUNKS_IMG + index(c)
                        pe.wait_ge(heads_act, n + 1)
                        pe.wait_ge(heads_dve, n + 1)
                        pe.wait_ge(k_rest, n + 1)
                        pe.wait_ge(rest_in[c[1]], (b * (CHUNKS_IMG // 2) + c[0] + 1) * len(LO_SP) * 16)
                    for l in range(p * PAIR, (p + 1) * PAIR):
                        last = split_product(scores_all[:H, l, 0:HG * H],
                                             lambda a, k: k_chunk[:, c[1], a, l * H:(l + 1) * H],
                                             lambda a, k: q_blocks[:, c[1], a, :, l * H:(l + 1) * H], 1)
                    last.then_inc(scores_done, 1)

                def values(half, j, first):
                    c, p = (half, j // PAIRS), j % PAIRS
                    n = b * CHUNKS_IMG + index(c)
                    if p == 0:
                        pe.wait_ge(v_in[c[1]], (b * (CHUNKS_IMG // 2) + half + 1) * 16)
                        if not first:
                            pe.wait_ge(o_taken, n - 1)
                    pe.wait_ge(probs_done, n * PAIRS + p + 1)
                    for l in range(p * PAIR, (p + 1) * PAIR):
                        for e in range(HG):
                            last = pe.matmul(o_bank[c[1]][e * HD:(e + 1) * HD, l * H:(l + 1) * H],
                                             v_chunk[:, c[1], l, e * HD:(e + 1) * HD],
                                             probs[:, l, e * H:(e + 1) * H], start=True, stop=True,
                                             skip_group_check=True)
                    last.then_inc(pv_done, 1)

                def down(u, bank_used, between=None):
                    if bank_used:
                        pe.wait_ge(final_done, strip_no(b, u) - 1)
                    for half in range(2):
                        if half and between:
                            between()
                        pe.wait_ge(act_lo[half], strip_no(b, u) + 1)
                        for t in range(T):
                            for k in range(half * KF // 2, (half + 1) * KF // 2):
                                for a, c in ((0, 0), (0, 1), (1, 0)):
                                    last = pe.matmul(down_bank[u[1]][:, t * C:(t + 1) * C],
                                                     act_t[:, a, k, t * P:(t + 1) * P], w_down[:, c, k, :],
                                                     start=(t == 0 and k == 0 and (a, c) == (0, 0)),
                                                     stop=(k == KF - 1 and (a, c) == (1, 0)),
                                                     skip_group_check=True)
                    last.then_inc(down_done, 1)

                def second_pass(s, inside):
                    if inside(0):
                        pe.wait_ge(ret_lo, strip_no(b, s) + 1)
                        for t in range(T):
                            last = split_product(proj_bank[s[1]][:, t * C:(t + 1) * C],
                                                 lambda a, k: ret_t[:, a, k, t * P:(t + 1) * P],
                                                 lambda c, k: w_proj[:, c, k, :], KC)
                        last.then_inc(proj_done, 1)
                    if inside(-1):
                        u = shifted(s, -1)
                        pe.wait_ge(norm2_done, strip_no(b, u) + 1)
                        transposes(u[1], norm_second)
                    if inside(-2):
                        down(shifted(s, -2), inside(-4))
                    if inside(-1):
                        u = shifted(s, -1)
                        pe.wait_ge(lo_done, ln_no(b, 1, u) + 1)
                        for n in range(KF):
                            last = split_product(up_bank[n // 2][:, n % 2 * STRIP:(n % 2 + 1) * STRIP],
                                                 lambda a, k: w_up[:, a, k, n * P:(n + 1) * P],
                                                 lambda c, k: h_t[:, u[1], c, k, :], KC)
                            if n % 2:
                                last.then_inc(up_done, 1)

                def two_chunks(half, first=False, final=False):
                    for j in range(2 * PAIRS):
                        if final and j == PAIRS:
                            one_slot(second_pass, 0, STRIPS)
                        if not final or j + 1 < 2 * PAIRS:
                            scores(half, j + 1)
                        values(half, j, first)

                scores(0, 0)
                pe.wait_ge(qk_stored, (b + 1) * STRIPS)
                two_chunks(0, first=True)
                with pe.Fori(1, CHUNKS_IMG // 2 - 1) as half:
                    two_chunks(half)
                two_chunks(CHUNKS_IMG // 2 - 1, final=True)

                run_slots(pe, second_pass, STRIPS, 4, 0, start=1, stop=STRIPS + 1)
                down(((STRIPS - 1) // 2, (STRIPS - 1) % 2), True,
                     (lambda: one_slot(lambda s, inside: first_pass(b + 1, s, inside), -1, STRIPS)) if more else None)
                if more:
                    one_slot(lambda s, inside: first_pass(b + 1, s, inside), 0, STRIPS)
                    pe.wait_ge(final_done, (b + 1) * STRIPS)

            for i in range(-1, 1):
                one_slot(lambda s, inside: first_pass(0, s, inside), i, STRIPS)
            run_images(pe, image, B)

        @block.scalar
        def _(act):
            def high_part(n, par):
                act.wait_ge(t_done, n + 1)
                act.activation(h_t[:, par, 0], t_bank[par][:, :].rearrange("p (k n) -> p k n", k=KC),
                               ACT.Copy).then_inc(hi_done, 1)

            def normalise_first(b, s):
                par = s[1]
                act.wait_ge(shift_done, strip_no(b, s) + 1)
                for t in range(T):
                    last = act.activation(norm_first[:, par, t], x_first[:, par, t], ACT.Identity,
                                          bias=shift[:, par, t:t + 1], scale=rstd[:, par, t:t + 1])
                last.then_inc(norm1_done, 1)

            def image(b, more):
                def round_q(m, c, first=False):
                    g, d = COMBOS[m]
                    n = chunk_no(b, m, c)
                    if not first:
                        act.wait_ge(scores_done, (n - 2) * PAIRS + 1)
                    act.activation(by_line(q_part(c, 0)), lines(q_img, g, d, c), ACT.Copy).then_inc(q_rounded, 1)

                def prepare(m, c, first=False):
                    g, d = COMBOS[m]
                    n = chunk_no(b, m, c)
                    if not first:
                        act.wait_ge(scores_done, (n - 1) * PAIRS)
                    act.activation(by_line(k_chunk[:, c[1], 0]), lines(k_img, g, d, c),
                                   ACT.Copy).then_inc(k_rounded, 1)
                    act.wait_ge(q_rounded, n + 1)
                    copy_heads(lambda o, i: act.activation(o, i, ACT.Copy), c, 0, HI_ACT)

                def rest_blocks(m, c):
                    act.wait_ge(q_rest, chunk_no(b, m, c) + 1)
                    copy_heads(lambda o, i: act.activation(o, i, ACT.Copy), c, 1,
                               LO_ACT[m % 2]).then_inc(heads_act, 1)

                def first_pass(s, inside):
                    if inside(1):
                        u = shifted(s, 1)
                        high_part(ln_no(b, 0, u), u[1])
                    if inside(2):
                        normalise_first(b, shifted(s, 2))
                    if inside(0) and not inside(1):
                        act.wait_ge(qk_stored, b * STRIPS + CH // STRIP + 1)
                        round_q(0, (0, 0), first=True)
                        prepare(0, (0, 0), first=True)
                    if inside(0):
                        for dst, src, signal, o in ((q_img, q_bank, q_done, 0), (k_img, k_bank, k_done, KC)):
                            if o and not inside(1):
                                rest_blocks(0, (0, 0))
                            act.wait_ge(signal, strip_no(b, s) + 1)
                            for g in range(KC):
                                last = act.activation(dst[:, g, ds(index(s) * STRIP, STRIP)],
                                                      src[s[1]][:, g * STRIP:(g + 1) * STRIP],
                                                      ACT.Identity, bias=qk_bias[:, o + g:o + g + 1])
                        last.then_inc(qk_stored, 1)
                        act.wait_ge(v_done, strip_no(b, s) + 1)
                        if inside(-2):
                            act.wait_ge(v_out[s[1]], landed(b, s) - 16)
                        act.activation(v_stage[:, s[1]], v_bank[s[1]][:, :].rearrange("p (t c) -> p t c", t=T),
                                       ACT.Copy).then_inc(v_copied, 1)

                run_slots(act, first_pass, STRIPS, 2, 2, start=0)

                act.wait_ge(qk_stored, (b + 1) * STRIPS)
                round_q(0, (0, 1), first=True)

                def store(m, c):
                    act.wait_ge(pv_done, (chunk_no(b, m, c) + 1) * PAIRS)
                    act.activation(lines(ret, *COMBOS[m], c), by_line(o_bank[c[1]][:, 0:CH]),
                                   ACT.Copy).then_inc(o_taken, 1)

                for m, (g, d) in enumerate(COMBOS):
                    def slot(c, inside, m=m, d=d):
                        nxt, after = (following(m, c, inside, k) if inside(0) else None for k in (1, 2))
                        if nxt:
                            prepare(*nxt, first=(m == 0 and not inside(-1)))
                        if after:
                            round_q(*after)
                        if nxt:
                            rest_blocks(*nxt)
                        if inside(-1) and m % 2 == 0:
                            if m and not inside(-2):
                                act.wait_ge(o_taken, b * CHUNKS_IMG + m * CHUNKS)
                            store(m, shifted(c, -1))
                        elif not inside(-1) and m % 2:
                            store(m - 1, LAST)

                    run_slots(act, slot, CHUNKS, 2, 2, start=0, stop=CHUNKS)

                assert 2 * STRIP <= 2 * CH
                act.wait_ge(o_taken, (b + 1) * CHUNKS_IMG - CHUNKS + 2)

                def second_pass(s, inside):
                    if inside(-1):
                        u = shifted(s, -1)
                        high_part(ln_no(b, 1, u), u[1])
                    if inside(1):
                        u = shifted(s, 1)
                        if inside(0):
                            act.wait_ge(proj_done, strip_no(b, u))
                        if inside(-1) and not inside(-2):
                            act.wait_ge(o_taken, (b + 1) * CHUNKS_IMG)
                        act.activation(ret_t[:, 0], tokens(ret, u), ACT.Copy).then_inc(ret_hi, 1)
                    if inside(-1):
                        n = strip_no(b, shifted(s, -1))
                        for half in range(2):
                            ks = range(half * KF // 2, (half + 1) * KF // 2)
                            act.wait_ge(up_done, 2 * n + half + 1)
                            for i, k in enumerate(ks):
                                last = act.activation(act_f[:, k], up_bank[half][:, i * STRIP:(i + 1) * STRIP],
                                                      ACT.Gelu, bias=up_bias[:, k:k + 1])
                            last.then_inc(gelu_done, 1)
                            act.wait_ge(gelu_done, 2 * n + half + 1)
                            act.activation(act_t[:, 0, ks[0]:ks[-1] + 1], act_f[:, ks[0]:ks[-1] + 1],
                                           ACT.Copy).then_inc(act_hi, 1)

                run_slots(act, second_pass, STRIPS, 1, 1)
                if more:
                    for u in range(2):
                        normalise_first(b + 1, (0, u))
                    high_part(ln_no(b + 1, 0, (0, 0)), 0)

            for u in range(2):
                normalise_first(0, (0, u))
            act.wait_ge(blocks_clear, 1)
            act.wait_ge(setup_ready, 1)
            high_part(0, 0)
            run_images(act, image, B)

        @block.vector
        def _(dve):
            links = [0]

            def link(ins):
                links[0] += 1
                ins.then_inc(setup_link, 1)
                dve.wait_ge(setup_link, links[0])

            def sums(pars, src):
                for u in range(pars.stop - pars.start):
                    for t in range(T):
                        dve.bn_stats(bn[:, pars.start + u, t], src[:, u, t]).then_inc(bn_done, 1)

            def moments(n, pars):
                k = pars.stop - pars.start
                dve.wait_ge(bn_done, (n + k) * T)
                dve.sem_inc(bn_seen, 1)
                for u in range(k):
                    for t in range(T):
                        dve.bn_aggr(mean_var[:, pars.start + u, t], bn[:, pars.start + u, t]).then_inc(mv_done, 1)
                dve.wait_ge(mv_done, (n + k) * T)
                var = mean_var[:, pars, :, 1]
                dve.tensor_scalar(var_eps[:, pars], var, EPS, None, ALU.add).then_inc(ve_done, k)
                dve.tensor_scalar(neg_half[:, pars], var, EPS, -0.5, ALU.add, ALU.mult).then_inc(ve_done, k)
                dve.wait_ge(ve_done, 2 * (n + k))
                y, t = rstd[:, pars], newton[:, pars]
                dve.tensor_scalar(y.bitcast(I32), var_eps[:, pars].bitcast(I32), -0.5, RSQRT_SEED,
                                  ALU.mult, ALU.add).then_inc(newton_step, k)
                done = 1
                for _ in range(NEWTON_STEPS):
                    for step in (lambda: dve.tensor_tensor(t, y, y, ALU.mult),
                                 lambda: dve.tensor_tensor(t, t, neg_half[:, pars], ALU.mult),
                                 lambda: dve.scalar_tensor_tensor(out=y, in0=t, scalar=1.5, in1=y,
                                                                  op0=ALU.add, op1=ALU.mult)):
                        dve.wait_ge(newton_step, n * (3 * NEWTON_STEPS + 1) + k * done)
                        step().then_inc(newton_step, k)
                        done += 1

            def statistics_first(b, s, both=False):
                k = 2 if both else 1
                n, pars = ln_no(b, 0, s), slice(s[1], s[1] + k)
                for u in range(k):
                    dve.wait_ge(xa_in[s[1] + u], landed(b, (s[0], s[1] + u)))
                sums(pars, x_first[:, pars])
                moments(n, pars)
                dve.wait_ge(newton_step, (n + k) * (3 * NEWTON_STEPS + 1))
                dve.scalar_tensor_tensor(out=shift[:, pars], in0=mean_var[:, pars, :, 0], scalar=-1.0,
                                         in1=rstd[:, pars], op0=ALU.mult, op1=ALU.mult).then_inc(shift_done, k)

            def normalise(n, par, src, x_norm):
                dve.wait_ge(newton_step, (n + 1) * (3 * NEWTON_STEPS + 1))
                for t in range(T):
                    last = dve.tensor_scalar(x_norm[:, par, t], src[:, t], mean_var[:, par, t, 0:1],
                                             rstd[:, par, t:t + 1], ALU.subtract, ALU.mult)
                last.then_inc(norm2_done, 1)

            def low_part(n, par):
                dve.wait_ge(hi_done, n + 1)
                dve.tensor_tensor(h_t[:, par, 1], t_bank[par][:, :].rearrange("p (k n) -> p k n", k=KC),
                                  h_t[:, par, 0].bitcast(F32), ALU.subtract).then_inc(lo_done, 1)

            def first_pass(b, s, inside):
                if inside(1):
                    u = shifted(s, 1)
                    low_part(ln_no(b, 0, u), u[1])
                if inside(3):
                    statistics_first(b, shifted(s, 3))

            def image(b, more):
                run_slots(dve, lambda s, inside: first_pass(b, s, inside), STRIPS, 0, 3, start=1)

                def start_strip(s, buffer_used):
                    n = strip_no(b, s)
                    dve.wait_ge(proj_done, n + 1)
                    dve.wait_ge(xb_done, n + 1)
                    if buffer_used:
                        dve.wait_ge(base_done, n - 1)
                    dve.tensor_tensor(x_mid[:, s[1]], proj_bank[s[1]][:, :].rearrange("p (t c) -> p t c", t=T),
                                      x_second[:, s[1]], ALU.add).then_inc(mid_done, 1)

                def start_sums(s):
                    dve.wait_ge(mid_done, strip_no(b, s) + 1)
                    sums(slice(s[1], s[1] + 1), x_mid[:, s[1]:s[1] + 1])

                def add(m, c):
                    dve.wait_ge(pv_done, (chunk_no(b, m, c) + 1) * PAIRS)
                    dve.tensor_tensor(lines(ret, *COMBOS[m], c), by_line(o_bank[c[1]][:, 0:CH]),
                                      lines(ret, *COMBOS[m], c), ALU.add).then_inc(o_taken, 1)

                def blocks(m, c, first=False):
                    n = chunk_no(b, m, c)
                    dve.wait_ge(q_rounded, n + 1)
                    if not first:
                        dve.wait_ge(scores_done, (n - 1) * PAIRS)
                    copy_heads(dve.tensor_copy, c, 0, HI_DVE)

                def rest_blocks(m, c):
                    dve.wait_ge(q_rest, chunk_no(b, m, c) + 1)
                    copy_heads(dve.tensor_copy, c, 1, LO_DVE[m % 2]).then_inc(heads_dve, 1)

                blocks(0, (0, 0), first=True)
                rest_blocks(0, (0, 0))
                for m, (g, d) in enumerate(COMBOS):
                    def slot(c, inside, m=m, g=g, d=d):
                        n = chunk_no(b, m, c)
                        if inside(1):
                            blocks(m, shifted(c, 1), first=(m == 0 and not inside(-1)))
                        elif m + 1 < len(COMBOS):
                            blocks(m + 1, (0, 0))
                        for p in range(PAIRS):
                            dve.wait_ge(scores_done, n * PAIRS + p + 1)
                            if m or inside(-1):
                                dve.wait_ge(pv_done, (n - 1) * PAIRS + p + 1)
                            pair = slice(p * PAIR, (p + 1) * PAIR)
                            dve.tensor_tensor(probs[:, pair], scores_all[:H, pair, 0:HG * H],
                                              decay[:, d, g].unsqueeze(1).broadcast_to([H, PAIR, HG * H]),
                                              ALU.mult).then_inc(probs_done, 1)
                            if p:
                                continue
                            if inside(1):
                                rest_blocks(m, shifted(c, 1))
                            elif m + 1 < len(COMBOS):
                                rest_blocks(m + 1, (0, 0))
                            if inside(-1) and m % 2:
                                if not inside(-2):
                                    dve.wait_ge(o_taken, b * CHUNKS_IMG + m * CHUNKS)
                                add(m, shifted(c, -1))
                            elif not inside(-1) and m and m % 2 == 0:
                                add(m - 1, LAST)
                            if m + 1 == len(COMBOS) and not inside(1):
                                start_strip((0, 0), False)
                                start_sums((0, 0))

                    run_slots(dve, slot, CHUNKS, 2, 1, start=0, stop=CHUNKS)
                def final_sum(u):
                    dve.wait_ge(down_done, strip_no(b, u) + 1)
                    dve.wait_ge(base_done, strip_no(b, u) + 1)
                    dve.tensor_tensor(y_stage[:, u[1]], down_bank[u[1]][:, :].rearrange("p (t c) -> p t c", t=T),
                                      y_stage[:, u[1]], ALU.add).then_inc(final_done, 1)

                def second_pass(s, inside):
                    if inside(0) and inside(-1):
                        start_strip(s, inside(-2))
                    if inside(-2):
                        low_act(dve, b, shifted(s, -2), 1)
                    if inside(-1):
                        u = shifted(s, -1)
                        low_part(ln_no(b, 1, u), u[1])
                    if inside(0):
                        if inside(-1):
                            start_sums(s)
                        moments(ln_no(b, 1, s), slice(s[1], s[1] + 1))
                        normalise(ln_no(b, 1, s), s[1], x_mid[:, s[1]], norm_second)
                    if inside(-2):
                        final_sum(shifted(s, -2))

                one_slot(second_pass, 0, STRIPS)
                add(len(COMBOS) - 1, LAST)
                run_slots(dve, second_pass, STRIPS, 2, 0, start=1, stop=STRIPS)
                tail = ((STRIPS - 1) // 2, (STRIPS - 1) % 2)
                low_act(dve, b, shifted(tail, -1), 1)
                low_part(ln_no(b, 1, tail), tail[1])
                if more:
                    statistics_first(b + 1, (0, 0), both=True)
                final_sum(shifted(tail, -1))
                low_act(dve, b, tail, 1)
                if more:
                    one_slot(lambda s, inside: first_pass(b + 1, s, inside), -1, STRIPS)
                final_sum(tail)
                if more:
                    one_slot(lambda s, inside: first_pass(b + 1, s, inside), 0, STRIPS)

            statistics_first(0, (0, 0), both=True)

            dve.wait_ge(ident_done, 1)
            dve.wait_ge(w_in, 14 * 16)
            for k in range(KC):
                last = dve.tensor_scalar(ln1_b_cols[:, k, :], ident[:, :], 0.0, b1[:, k:k + 1], ALU.mult, ALU.add)
            last.then_inc(setup_v, 1)
            for raw, w, gain in ((raw_qkv, w_qkv, g1), (raw_up, w_up, g2)):
                for k in range(KC):
                    link(dve.tensor_scalar(w[:, 0, k], raw[:, k], gain[:, k:k + 1], None, ALU.mult))
                    dve.scalar_tensor_tensor(out=w[:, 1, k], in0=raw[:, k], scalar=gain[:, k:k + 1],
                                             in1=w[:, 0, k].bitcast(F32), op0=ALU.mult, op1=ALU.subtract)
            link(dve.tensor_tensor(proj_scaled, raw_proj, gamma_row.unsqueeze(1).broadcast_to([P, KC, C]), ALU.mult))
            for raw, w in ((proj_scaled, w_proj), (raw_down, w_down)):
                link(dve.tensor_copy(w[:, 0], raw))
                dve.tensor_tensor(w[:, 1], raw, w[:, 0].bitcast(F32), ALU.subtract)
            dve.tensor_tensor(proj_bias[:, :], proj_bias[:, :], gamma_row, ALU.mult)
            dve.wait_ge(setup_pe, 1)
            dve.tensor_tensor(qk_bias[:, :], bank[4][:, 0:2 * KC], raw_qk_bias, ALU.add)
            dve.tensor_tensor(up_bias[:, :], bank[4][:, 2 * KC:2 * KC + KF], raw_up_bias, ALU.add)
            dve.tensor_tensor(v_bias[:, :], bank[5][:, 0:C], v_bias[:, :], ALU.add)
            dve.wait_ge(setup_pe, 2)
            for d in range(2):
                for g in range(KC):
                    last = dve.tensor_scalar(decay[:, d, g], bank[2 * d + g][:H, 0:HG * H], 0.5, None, ALU.mult)
            last.then_inc(setup_ready, 1)
            dve.wait_ge(setup_ready, 1)

            for i in range(-1, 1):
                one_slot(lambda s, inside: first_pass(0, s, inside), i, STRIPS)
            run_images(dve, image, B)


NAMES = ("x", "L0_conv_decay_h", "L0_conv_decay_w", "L0_conv_qkv_w", "L0_conv_qkv_b", "L0_conv_proj_w",
         "L0_conv_proj_b", "L0_conv_ln1_g", "L0_conv_ln1_b", "L0_conv_ln2_g", "L0_conv_ln2_b",
         "L0_conv_ffn_w1", "L0_conv_ffn_b1", "L0_conv_ffn_w2", "L0_conv_ffn_b2", "L0_conv_gamma")


def kernel(**inputs):
    import numpy as np
    import concourse.bacc as bacc
    from concourse.bass_utils import run_bass_kernel_spmd

    nc = bacc.Bacc("TRN2", target_bir_lowering=False, num_devices=1)
    arrays, args = {}, []
    for name in NAMES:
        a = np.ascontiguousarray(inputs[name])
        arrays[f"in_{name}"] = a
        args.append(nc.dram_tensor(f"in_{name}", a.shape, F32, kind="ExternalInput").ap())
    shape = inputs["x"].shape
    v_rows = nc.dram_tensor("v_rows", shape, F32, kind="Internal").ap()
    out = nc.dram_tensor("out", shape, F32, kind="ExternalOutput").ap()
    build(nc, *args, v_rows, out)
    result = run_bass_kernel_spmd(nc, [arrays], core_ids=[0])
    return result.results[0]["out"]
```
